# Optimizing a Trainium2 kernel written in Bass

```python
import numpy as np
import jax
import jax.numpy as jnp

def _softmax(x, axis=-1):
    return jax.nn.softmax(x, axis=axis)

def _gelu(x):
    return jax.nn.gelu(x, approximate=True)

def _silu(x):
    return jax.nn.silu(x)

def _sigmoid(x):
    return jax.nn.sigmoid(x)

def _layernorm(x, axis=-1, eps=1e-05):
    m = jnp.mean(x, axis=axis, keepdims=True)
    v = jnp.var(x, axis=axis, keepdims=True)
    return (x - m) / jnp.sqrt(v + eps)

def _scatter_add(tgt, idx, src, axis=0):
    return tgt.at[idx].add(src)

def _segment_sum(src, seg, n):
    return jax.ops.segment_sum(src, seg, n)
kernel_name = 'mk_prb_d1_jaxref_r8_bf320b'

def setup_inputs(seed: int=0):
    np.random.seed(seed)
    _w = jnp.asarray

    def _L0_attn_setup():
        import jax, jax.numpy as jnp
        import numpy as np
        B, S, D, H = (2, 256, 256, 16)
        HD = D // H
        NEG = jnp.float32(-1000000000.0)
        key = jax.random.key(seed)
        ks = jax.random.split(key, 6)
        slopes = np.array([2 ** (-8.0 * (i + 1) / H) for i in range(H)], dtype=np.float32)
        return {'hidden_states': jax.random.normal(ks[0], (B, S, D), jnp.float32), 'qkv_w': jax.random.normal(ks[1], (3 * D, D), jnp.float32) * (1.0 / np.sqrt(D)), 'qkv_b': jax.random.normal(ks[2], (3 * D,), jnp.float32) * 0.01, 'out_w': jax.random.normal(ks[3], (D, D), jnp.float32) * (1.0 / np.sqrt(D)), 'out_b': jax.random.normal(ks[4], (D,), jnp.float32) * 0.01, 'alibi_slopes': jnp.asarray(slopes)}
    _L0_attn_in = _L0_attn_setup()

    def _L0_ffn_setup():
        import jax, jax.numpy as jnp
        import numpy as np
        B, S, H = (1, 128, 256)
        F = 128
        E = 16
        K = 2
        NS = 1
        ROUTE_SCALE = 1.0
        key = jax.random.key(seed)
        ks = jax.random.split(key, 8)

        def w(k, shape, fan_in):
            return jax.random.normal(k, shape, jnp.float32) * fan_in ** (-0.5)
        return {'hidden_states': jax.random.normal(ks[0], (B, S, H), jnp.float32), 'gate_w': w(ks[1], (H, E), H), 'expert_bias': jnp.zeros((E,), jnp.float32), 'shared_gate_w': w(ks[2], (H, F * NS), H), 'shared_up_w': w(ks[3], (H, F * NS), H), 'shared_down_w': w(ks[4], (F * NS, H), F * NS), 'experts_gate_up': w(ks[5], (E, H, 2 * F), H), 'experts_down': w(ks[6], (E, F, H), F)}
    _L0_ffn_in = _L0_ffn_setup()
    _d = {'L0_attn_hidden_states': _L0_attn_in['hidden_states'], 'L0_attn_qkv_w': _L0_attn_in['qkv_w'], 'L0_attn_qkv_b': _L0_attn_in['qkv_b'], 'L0_attn_out_w': _L0_attn_in['out_w'], 'L0_attn_out_b': _L0_attn_in['out_b'], 'L0_attn_alibi_slopes': _L0_attn_in['alibi_slopes'], 'L0_ffn_gate_w': _L0_ffn_in['gate_w'], 'L0_ffn_expert_bias': _L0_ffn_in['expert_bias'], 'L0_ffn_shared_gate_w': _L0_ffn_in['shared_gate_w'], 'L0_ffn_shared_up_w': _L0_ffn_in['shared_up_w'], 'L0_ffn_shared_down_w': _L0_ffn_in['shared_down_w'], 'L0_ffn_experts_gate_up': _L0_ffn_in['experts_gate_up'], 'L0_ffn_experts_down': _L0_ffn_in['experts_down']}
    _x0 = _d['L0_attn_hidden_states']
    _d['L0_attn_hidden_states'] = jax.random.normal(jax.random.fold_in(jax.random.key(seed), 1), (2, 1024, 256), dtype=_x0.dtype)
    del _x0
    return _d

def reference(L0_attn_hidden_states, L0_attn_qkv_w, L0_attn_qkv_b, L0_attn_out_w, L0_attn_out_b, L0_attn_alibi_slopes, L0_ffn_gate_w, L0_ffn_expert_bias, L0_ffn_shared_gate_w, L0_ffn_shared_up_w, L0_ffn_shared_down_w, L0_ffn_experts_gate_up, L0_ffn_experts_down):

    def _L0_attn_ref(hidden_states, qkv_w, qkv_b, out_w, out_b, alibi_slopes):
        import jax, jax.numpy as jnp
        import numpy as np
        B, S, D, H = (2, 256, 256, 16)
        HD = D // H
        NEG = jnp.float32(-1000000000.0)
        b, s, d = hidden_states.shape
        qkv = hidden_states @ qkv_w.T + qkv_b
        q, k, v = jnp.split(qkv, 3, axis=-1)
        q = q.reshape(b, s, H, HD)
        k = k.reshape(b, s, H, HD)
        v = v.reshape(b, s, H, HD)
        scale = 1.0 / np.sqrt(HD)
        scores = jnp.einsum('bqhd,bkhd->bhqk', q, k) * scale
        pos = jnp.arange(s)
        rel = (pos[None, :] - pos[:, None]).astype(jnp.float32)
        bias = alibi_slopes[:, None, None] * rel
        causal = pos[None, :] <= pos[:, None]
        scores = jnp.where(causal[None, None], scores + bias[None], NEG)
        attn = jax.nn.softmax(scores, axis=-1)
        out = jnp.einsum('bhqk,bkhd->bqhd', attn, v).reshape(b, s, d)
        out = out @ out_w.T + out_b
        return out

    def _L0_ffn_ref(hidden_states, gate_w, expert_bias, shared_gate_w, shared_up_w, shared_down_w, experts_gate_up, experts_down):
        import jax, jax.numpy as jnp
        import numpy as np
        B, S, H = (1, 128, 256)
        F = 128
        E = 16
        K = 2
        NS = 1
        ROUTE_SCALE = 1.0
        b, s, h = hidden_states.shape
        x = hidden_states.reshape(-1, h)
        T = x.shape[0]
        router_logits = (x @ gate_w).astype(jnp.float32)
        scores = jax.nn.sigmoid(router_logits)
        _, selected = jax.lax.top_k(scores + expert_bias[None, :], K)
        top_scores = jnp.take_along_axis(scores, selected, axis=1)
        top_scores = top_scores / (top_scores.sum(-1, keepdims=True) + 1e-20)
        top_scores = top_scores * ROUTE_SCALE
        shared = jax.nn.silu(x @ shared_gate_w) * (x @ shared_up_w) @ shared_down_w
        comb = jnp.zeros((T, E), jnp.float32).at[jnp.arange(T)[:, None], selected].add(top_scores)
        routed = jnp.zeros_like(x)
        for e in range(E):
            gu = x @ experts_gate_up[e]
            g, u = jnp.split(gu, 2, axis=-1)
            routed = routed + comb[:, e:e + 1] * (jax.nn.silu(g) * u @ experts_down[e])
        return (shared + routed).reshape(b, s, h)
    x = L0_attn_hidden_states
    xn = _layernorm(x, axis=-1)
    x = x + _L0_attn_ref(xn, L0_attn_qkv_w, L0_attn_qkv_b, L0_attn_out_w, L0_attn_out_b, L0_attn_alibi_slopes) + _L0_ffn_ref(xn, L0_ffn_gate_w, L0_ffn_expert_bias, L0_ffn_shared_gate_w, L0_ffn_shared_up_w, L0_ffn_shared_down_w, L0_ffn_experts_gate_up, L0_ffn_experts_down)
    return x

_drawn_inputs = setup_inputs


def setup_inputs(seed=0):
    import zlib

    import numpy as np

    out = dict(_drawn_inputs(seed))
    spreads = {'L0_ffn_expert_bias': (0.0, 0.1)}
    factors = {'L0_attn_qkv_b': 5.958, 'L0_attn_out_b': 7.617}
    for name, (base, spread) in spreads.items():
        noise = np.random.default_rng([zlib.crc32(name.encode()), seed]).standard_normal(out[name].shape)
        drawn = base * np.exp(spread * noise) if base else spread * noise
        out[name] = jnp.asarray(drawn.astype(out[name].dtype))
    for name, factor in factors.items():
        out[name] = (out[name] * factor).astype(out[name].dtype)
    return out
```

```python
from contextlib import ExitStack

import numpy as np

import concourse.bass as bass
import concourse.mybir as mybir

F32 = mybir.dt.float32
F32R = mybir.dt.float32r
BF16 = mybir.dt.bfloat16
I32 = mybir.dt.int32
ALU = mybir.AluOpType
ACT = mybir.ActivationFunctionType
AX = mybir.AxisListType

P = 128
B, S, D, H = 2, 1024, 256, 16
HD = D // H
T = B * S
TT = T // P
KC = D // P
E, F, K_TOP = 16, 128, 2
NT = (K_TOP * T + E * (P - 1)) // P + 1
NT = -(-NT // 4) * 4
SLOTS = NT * P
HG = 4
NG = B * H // HG
QT = S // P
CH = 512
NEG = -1.0e30
LN_EPS = 1e-5

Q_PARTS = (0, 0, 0, 1, 1, 2)
K_PARTS = (0, 1, 2, 0, 1, 0)
AUX0 = 6 * HD
N_ALIBI = 12
N0 = AUX0 + N_ALIBI
K_MAX = N0
K_EXP = N0 + 3
N_AUX = K_EXP - AUX0
AUXP = H // 2 * N_AUX

STEPS = [(qc, kb) for qc in range(2) for kb in range(4 * qc + 4)]
NS = len(STEPS)


def max_pieces():
    out = [(0, 0, 4), (1, 0, 2), (1, 2, 2)]
    for qt in range(2, QT):
        out += [(qt, j, 1) for j in range(HG)]
    return out


PIECES = max_pieces()
NP = len(PIECES) + 1
EARLY = 7


def schedule():
    items = [("exp", s, j) for s in range(NS) for j in range(HG)]
    exp_cost = [(CH - max(0, STEPS[s][1] * P - STEPS[s][0] * CH)) + 230 for _, s, _ in items]
    pieces = [(1, p) for p in range(EARLY, NP)] + [(2, p) for p in range(EARLY)]
    max_cost = [(1 + PIECES[p][0]) * P * PIECES[p][2] + 200 if p < NP - 1 else 700 for _, p in pieces]
    out, at, done, due = [], 0, 0, 0
    for item, cost in zip(items, exp_cost):
        out.append(item)
        due += cost / sum(exp_cost)
        while at < len(pieces) and done + max_cost[at] / sum(max_cost) / 2 <= due:
            if pieces[at][0] == 2 and item[1] < EARLY_STEP:
                break
            out.append(("max", *pieces[at]))
            done += max_cost[at] / sum(max_cost)
            at += 1
        if item[2] == OUT_AFTER:
            out.append(("out", item[1]))
    out += [("max", *x) for x in pieces[at:]]
    return out


EARLY_STEP = 10
OUT_AFTER = 2
ORDER = schedule()


def constants():
    bf = mybir.dt.np(BF16)
    k = np.arange(P)
    above = np.where(k[None, :] > k[:, None], NEG, 0.0)
    pos = np.arange(S)
    a, b, one = pos // 8 * 8, pos % 8, np.ones(S)
    tq = np.stack([one, a, one, b] * 3 + [one] * 3)
    tk = np.stack([a, one, b, one] * 3 + [one] * 3)
    coef = np.zeros((N_AUX, 2, 4), np.float32)
    for r in range(N_ALIBI):
        if r % 2 == 0:
            coef[r, 0, r // 4] = 1
            coef[r, 1, 3] = 1
        else:
            coef[r, 0, 3] = 1
            coef[r, 1, r // 4] = -1
    coef[N_ALIBI:, 1, 3] = 1
    e = np.arange(E)
    row = np.concatenate([E - e, (e[None, :] < e[:, None]).ravel(), np.tile(P * e, E), np.repeat(np.arange(NT), E)])
    sel = np.zeros((P, P), np.float32)
    for m in range(P):
        sel[m // 32 * 32 + HD, m] = 1
    lower = (k[:, None] < k[None, :]).astype(np.float32)
    return {
        "c_ident": np.eye(P, dtype=np.float32),
        "c_bf": np.concatenate([np.eye(P), above, above.T, lower, np.ones((P, P))], 1).astype(bf),
        "c_pos": np.tile(np.concatenate([tq, tk], 1), (H // 2, 1)).astype(bf),
        "c_coef": np.tile(coef.reshape(N_AUX, 8), (H // 2, 1)),
        "c_sel": sel,
        "c_row": row.astype(np.float32),
    }


def build(nc, x, qkv_w, qkv_b, out_w, out_b, slopes, gate_w, ebias, sg_w, su_w, sd_w, e_gu, e_dn,
          c_ident, c_bf, c_pos, c_coef, c_sel, c_row, y):
    ctx = ExitStack()
    with ctx:
        def sb(name, shape, dt=F32):
            return ctx.enter_context(nc.sbuf_tensor(name, shape, dt))

        def sem(name):
            return ctx.enter_context(nc.semaphore(name))

        x_sb = sb("x_sb", [P, TT, D])
        wo_t = sb("wo_t", [P, H // HG, D])
        ident = sb("ident", [P, P])
        cbf = sb("cbf", [P, 5 * P], BF16)
        sel = sb("sel", [P, P])
        v_sb = sb("v_sb", [P, NG, QT, HG * HD])
        yg = sb("yg", [P, 4, D])
        mx = sb("mx", [P, 2, HG * QT])
        nr = sb("nr", [HG * QT, 2, 3, P], BF16)
        nrf = sb("nrf", [HG * QT, 2, P])
        rden = sb("rden", [P, NG * 2 * 4, HG])
        slot_i = sb("slot_i", [P, K_TOP, TT], I32)
        eid = sb("eid", [P, NT], I32)
        gates = sb("gates", [P, K_TOP, TT])
        mv_pad = sb("mv_pad", [P, 4])
        vg = sb("vg", [P, 2, QT, HG, 32])
        ps = ctx.enter_context(nc.psum_tensor("ps", [P, 8 * CH], F32))

        with nc.sbuf_tensor("xh", [P, KC, T], F32R) as xh, nc.sbuf_tensor("xl", [P, KC, T], F32R) as xl:
            pass
        with nc.sbuf_tensor("rden_x", [P, NG * QT, HG, 32], F32) as rden_x:
            pass
        qs = sb("qs", [P, 2, HG, S], BF16)
        ks = sb("ks", [P, 2, HG, S], BF16)
        with ExitStack() as early:
            def tmp(name, shape, dt=F32):
                return early.enter_context(nc.sbuf_tensor(name, shape, dt))

            xn = tmp("xn", [P, TT, D])
            w_gu = tmp("w_gu", [P, E, KC, 2 * F])
            wh = tmp("wh", [P, KC, 3 * D], F32R)
            wl = tmp("wl", [P, KC, 3 * D], F32R)
            gw = tmp("gw", [P, KC, E])
            gwh = tmp("gwh", [P, KC, E], F32R)
            gwl = tmp("gwl", [P, KC, E], F32R)
            ws = tmp("ws", [P, KC, 2, F])
            wsh = tmp("wsh", [P, KC, 2, F], F32R)
            wsl = tmp("wsl", [P, KC, 2, F], F32R)
            wsd = tmp("wsd", [P, D])
            qkb = tmp("qkb", [P, 4])
            qkb_in = tmp("qkb_in", [P, 4])
            vb = tmp("vb", [P, D])
            eb = tmp("eb", [P, E])
            row = tmp("row", [P, E + 2 * E * E + NT * E])
            eps_t = tmp("eps_t", [P, 1])
            stats = tmp("stats", [P, TT, 6])
            mv = tmp("mv", [P, TT, 2])
            std = tmp("std", [P, TT])
            rstd = tmp("rstd", [P, TT])
            coef_t = tmp("coef_t", [AUXP, 8])
            slope_in = tmp("slope_in", [AUXP, 2])
            sl = tmp("sl", [AUXP, 3, 2], BF16)
            slr = tmp("slr", [AUXP, 3, 2])
            cq = tmp("cq", [AUXP, 2, 2])
            prob = tmp("prob", [P, TT, E])
            biased = tmp("biased", [P, TT, E])
            rt = tmp("rt", [P, TT, E])
            pick = tmp("pick", [P, K_TOP, TT, E])
            picked = tmp("picked", [P, TT, E], BF16)
            top = tmp("top", [P, 8, TT])
            cnt = tmp("cnt", [P, 4, E])
            etab = tmp("etab", [P, NT * E])
            slot_f = tmp("slot_f", [P, K_TOP, TT])
            eid_f = tmp("eid_f", [P, NT])
            y_out = tmp("y_out", [P, 4, D])
            ht = tmp("ht", [P, 2, P])
            with ExitStack() as first:
                def now(name, shape, dt=F32):
                    return first.enter_context(nc.sbuf_tensor(name, shape, dt))

                part_h = now("part_h", [P, 2, CH], BF16)
                part_m = now("part_m", [P, 2, CH], BF16)
                part_l = now("part_l", [P, 2, CH], BF16)
                part_r = now("part_r", [P, 2, CH])
            th = tmp("th", [P, 2, CH])
            hsh = tmp("hsh", [P, 2, CH])
            with ExitStack() as first:
                def now(name, shape, dt=F32):
                    return first.enter_context(nc.sbuf_tensor(name, shape, dt))

                w_nat = now("w_nat", [P, 6, D])
                wo_nat = now("wo_nat", [P, KC, H // HG, HG, 32])
                pos_t = now("pos_t", [AUXP, 2 * S], BF16)
                aux = now("aux", [AUXP, 4, S], BF16)
            w_dn = tmp("w_dn", [P, E, D])
            x_in = tmp("x_in", [P, 4, D])
            xt = tmp("xt", [P, 2, KC, P])
            te_h = tmp("te_h", [P, 2, F])
            hh = tmp("hh", [P, 2, F])
        pt = sb("pt", [P, 2, HG, CH])
        ot = sb("ot", [P, NG, S])

        def bank(n, w=CH, m=P):
            return ps[0:m, n * CH:n * CH + w]

        idb = cbf[:, 0:P]
        mask_q = cbf[:, P:2 * P]
        mask_k = cbf[:, 2 * P:3 * P]

        qkd = nc.dram_tensor("qk_parts", [2, NG, 3, HD, HG, S], BF16, kind="Internal").ap()
        auxd = nc.dram_tensor("aux_rows", [2, NG, HG, N_AUX, S], BF16, kind="Internal").ap()
        xsd = nc.dram_tensor("sorted_tokens", [SLOTS, D], F32, kind="Internal").ap()
        ysd = nc.dram_tensor("sorted_outputs", [SLOTS, D], F32, kind="Internal").ap()

        s_x = [sem(f"x_loaded{i}") for i in range(4)]
        s_w = sem("w_loaded")
        s_c = sem("consts_loaded")
        s_wo = sem("wo_loaded")
        s_ws = sem("small_weights_loaded")
        s_wgu = sem("expert_gate_up_loaded")
        s_wdn = sem("expert_down_loaded")
        s_zero = sem("zeroed")
        s_clear = sem("slots_cleared")
        s_pool = sem("pool_step")
        s_ln = sem("ln_step")
        s_std = sem("std_ready")
        s_qkb = sem("qk_bias_ready")
        s_small = sem("small_weights_high")
        s_smalll = sem("small_weights_low")
        s_xn = sem("xn_ready")
        s_job = sem("job_ready")
        s_hi = sem("hi_ready")
        s_free = sem("bank_freed")
        s_res = sem("residual_ready")
        s_mid = sem("mid_ready")
        s_parts = [[sem(f"part{k}_stored{i}") for i in range(2)] for k in range(3)]
        s_aux = sem("aux_ready")
        s_auxst = sem("aux_stored")
        s_prob = sem("router_exp_ready")
        s_r = sem("router_step")
        s_picked = sem("picked_ready")
        s_rank = sem("ranks_ready")
        s_slot = sem("slots_ready")
        s_scat = sem("tokens_sorted")
        s_g1 = sem("shared_hidden_ready")
        s_th = sem("shared_tanh_ready")
        s_ta = sem("shared_step")
        s_h = sem("shared_h_ready")
        s_sh = sem("shared_out_ready")
        s_sha = sem("shared_added")
        s_xin = [sem(f"tile_loaded{i}") for i in range(4)]
        s_tx = sem("tile_transposed")
        s_xt = sem("tile_evacuated")
        s_gu = sem("tile_gate_up_ready")
        s_tt = sem("tile_tanh_ready")
        s_tstep = sem("tile_step")
        s_hh = sem("tile_h_ready")
        s_tht = sem("tile_h_transposed")
        s_ht = sem("tile_h_evacuated")
        s_dn = sem("tile_out_ready")
        s_yo = sem("tile_out_evacuated")
        s_ys = [sem(f"tile_out_stored{i}") for i in range(4)]
        s_ga = [sem(f"rows_gathered{i}") for i in range(4)]
        s_gw = sem("rows_weighed")
        s_gad = sem("rows_added")
        s_ld = [[[sem(f"{side}_half{half}_loaded{p}") for p in range(2)] for half in range(2)] for side in "qk"]
        s_vg = sem("vg_ready")
        s_mxr = sem("max_scores_ready")
        s_mxf = sem("max_slot_freed")
        s_nstep = sem("neg_step")
        s_n = sem("neg_ready")
        s_nl = [sem(f"neg_loaded{p}") for p in range(2)]
        s_st = sem("scores_ready")
        s_exp = sem("exp_done")
        s_pv = sem("pv_done")
        s_ev = sem("out_evacuated")
        s_sum = sem("sums_transposed")
        s_rden = sem("sums_inverted")
        s_rx = sem("inverted_sums_spread")
        s_bc = sem("sum_broadcast")
        s_dv = sem("divided")
        s_pr = sem("projected")
        s_add = sem("added")
        s_y = sem("y_stored")

        block = ctx.enter_context(nc.Block())

        JOBS = ([("w", kc, c) for kc in range(KC) for c in range(3)] + [("o", oc, 0) for oc in range(2)]
                + [("x", n, 0) for n in range(TT // 2)] + [("r", 0, 0)]
                + [("qk", fc, tc) for tc in range(2) for fc in range(4)] + [("k", 0, 0)]
                + [("qk", fc, tc) for tc in range(2, 4) for fc in range(4)] + [("v", n, 0) for n in range(TT // 2)])
        at = {kind: next(n for n, j in enumerate(JOBS) if j[0] == kind) for kind in ("x", "r", "v")}
        X0, R0, V0 = at["x"], at["r"], at["v"]
        QKJ = [n for n, j in enumerate(JOBS) if j[0] == "qk"]
        NJ, NQK = len(JOBS), len(QKJ)
        HI_OF = [sum(j[0] in ("w", "x", "qk") for j in JOBS[:n + 1]) for n in range(NJ)]
        OUT_BANK = 3
        EXP_CREDIT, PV_CREDIT, MX_CREDIT = 3, 2, 2
        DMA = 16
        N_CONST = 11
        LOADS = 4
        SC = HD ** -0.5

        @block.sync
        def _(sp):
            sp.dma_start(w_nat[:, :, :], qkv_w.rearrange("(c p) k -> p c k", p=P)).then_inc(s_w, DMA)
            xv = x.rearrange("b (t p) d -> p (b t) d", p=P)
            for n in range(4):
                sp.dma_start(x_sb[:, 4 * n:4 * n + 4, :], xv[:, 4 * n:4 * n + 4, :]).then_inc(s_x[n], DMA)
            sp.wait_ge(s_zero, 3)
            xz = xsd.rearrange("(p k) d -> p (k d)", p=P)
            for n in range(NT // 4):
                sp.dma_start(xz[:, n * 4 * D:(n + 1) * 4 * D], y_out[:, :, :].rearrange("p k d -> p (k d)")
                             ).then_inc(s_clear, DMA)
            sp.dma_start(w_gu[:, :, :, :], e_gu.rearrange("e (c p) f -> p e c f", p=P)).then_inc(s_wgu, DMA)
            for n in range(4):
                side, half = n // 2, n % 2
                sp.wait_ge(s_aux, n + 1)
                for b in range(B):
                    sp.dma_start(auxd[side, b * 4 + 2 * half:b * 4 + 2 * half + 2].rearrange("g j r s -> (g j r) s"),
                                 aux[:, n, :]).then_inc(s_auxst, DMA)
            for i in range(NQK):
                _, fc, tc = JOBS[QKJ[i]]
                side, half = fc // 2, fc % 2
                b, s0 = tc // 2, tc % 2 * CH
                for part, buf in enumerate((part_h, part_m, part_l)):
                    if part == 0:
                        sp.wait_ge(s_hi, HI_OF[QKJ[i]])
                    else:
                        sp.wait_ge((s_mid, s_free)[part - 1], (i, QKJ[i])[part - 1] + 1)
                    g0 = b * 4 + 2 * half
                    for g in range(2):
                        dst = qkd[side, g0 + g, part, :, :, s0:s0 + CH].rearrange("d j s -> j d s")
                        sp.dma_start(dst, buf[g * P // 2:(g + 1) * P // 2, i % 2, :]
                                     ).then_inc(s_parts[part][i % 2], DMA)
            sp.wait_ge(s_job, X0)
            sp.wait_ge(s_auxst, 4 * B * DMA)
            sp.dma_start(w_dn[:, :, :], e_dn.rearrange("e f d -> f e d")).then_inc(s_wdn, DMA)
            sp.wait_ge(s_scat, K_TOP * TT * DMA)

            def load_tile(k, u):
                sp.dma_start(x_in[:, u, :], xsd[bass.ds(k * P, P), :]).then_inc(s_xin[u], DMA)

            def store_tile(k, u):
                sp.wait_ge(s_yo, k + 1)
                sp.dma_start(ysd[bass.ds(k * P, P), :], y_out[:, u, :]).then_inc(s_ys[u], DMA)

            for k in range(4):
                load_tile(k, k)
            for stored in s_parts:
                for i in range(2):
                    sp.wait_ge(stored[i], DMA * NQK)
            sp.wait_ge(s_sh, TT // 2)

            def load(side, g, par, half):
                dst, order, done = (qs, ks)[side], (Q_PARTS, K_PARTS)[side], s_ld[side][half][par]
                cols = slice(half * CH, (half + 1) * CH)
                for t0, n in ((0, 3), (3, 2), (5, 1)):
                    p0 = order[t0]
                    if side == 0:
                        src = qkd[0, bass.ds(g, 1), p0:p0 + 1, :, :, cols].rearrange("g n d j s -> (g n) d j s")
                        src = src.broadcast_to([n, HD, HG, CH])
                    else:
                        src = qkd[1, bass.ds(g, 1), 0:n, :, :, cols].rearrange("g n d j s -> (g n d) j s")
                    sp.dma_start(dst[HD * t0:HD * (t0 + n), par, :, cols], src).then_inc(done, DMA)
                rows = (N_ALIBI, N_AUX)[side]
                sp.dma_start(dst[AUX0:AUX0 + rows, par, :, cols],
                             auxd[side, bass.ds(g, 1), :, 0:rows, cols].rearrange("g j r s -> r (g j) s")
                             ).then_inc(done, DMA)

            def store_neg(g, par):
                sp.wait_ge(s_n, g + 1)
                for r in range(3):
                    sp.dma_start(qs[N0 + r:N0 + r + 1, par, :, :].rearrange("o j (t c) -> o (j t) c", c=P),
                                 nr[:, par, r, :]).then_inc(s_nl[par], DMA)

            for g in range(2):
                for half in range(2):
                    load(0, g, g, half)
                    load(1, g, g, half)
            with sp.Fori(0, NT // 4 - 1) as i:
                for u in range(4):
                    sp.wait_ge(s_tx, i * 4 + u + 1)
                    load_tile(i * 4 + u + 4, u)
                    store_tile(i * 4 + u, u)
            for u in range(4):
                store_tile(NT - 4 + u, u)
            store_neg(0, 0)

            def group(g, par, ahead):
                if ahead >= 2:
                    sp.wait_ge(s_st, g * (HG * NS) + HG * 4)
                    load(0, g + 2, par, 0)
                    sp.wait_ge(s_st, g * (HG * NS) + HG * 8)
                    load(1, g + 2, par, 0)
                if ahead >= 1:
                    store_neg(g + 1, 1 - par)
                if ahead >= 2:
                    sp.wait_ge(s_st, g * (HG * NS) + HG * NS)
                    load(0, g + 2, par, 1)
                    load(1, g + 2, par, 1)

            with sp.Fori(0, NG // 2 - 1) as i:
                group(i * 2, 0, 2)
                group(i * 2 + 1, 1, 2)
            group(NG - 2, 0, 1)
            yv = y.rearrange("b (t p) d -> p (b t) d", p=P)
            for t in range(TT):
                sp.wait_ge(s_add, t + 1)
                sp.dma_start(yv[:, t, :], x_sb[:, t, :]).then_inc(s_y, DMA)
            sp.wait_ge(s_y, DMA * TT)

        @block.gpsimd
        def _(pool):
            g_ = nc.gpsimd
            step = [0]

            def link(ins):
                ins.then_inc(s_pool, 1)
                step[0] += 1
                pool.wait_ge(s_pool, step[0])

            g_.memset(y_out[:, :, :], 0.0).then_inc(s_zero, 1)
            g_.memset(wo_nat[:, :, :, :, :], 0.0).then_inc(s_zero, 1)
            g_.memset(eps_t[:, :], LN_EPS).then_inc(s_zero, 1)
            g_.memset(mv_pad[:, 0:1], 0.0).then_inc(s_pv, PV_CREDIT)
            g_.memset(mv_pad[:, 1:2], 0.0).then_inc(s_ev, 1)
            link(g_.memset(vg[:, :, :, :, :], 0.0))
            link(g_.memset(vg[:, :, :, :, HD:HD + 1], 1.0))
            pool.wait_ge(s_c, DMA * N_CONST)
            link(g_.tensor_copy(sl[:, 0, :], slope_in[:, :]))
            link(g_.tensor_tensor(slr[:, 1, :], slope_in[:, :], sl[:, 0, :], ALU.subtract))
            link(g_.tensor_copy(sl[:, 1, :], slr[:, 1, :]))
            link(g_.tensor_tensor(slr[:, 2, :], slr[:, 1, :], sl[:, 1, :], ALU.subtract))
            link(g_.tensor_copy(sl[:, 2, :], slr[:, 2, :]))
            for side in range(2):
                c = coef_t[:, 4 * side:4 * side + 4]
                link(g_.tensor_scalar(cq[:, side, :], sl[:, 0, :], c[:, 0:1], c[:, 3:4], ALU.mult, ALU.add))
                for k in (1, 2):
                    link(g_.tensor_scalar(slr[:, 0, :], sl[:, k, :], c[:, k:k + 1], None, ALU.mult))
                    link(g_.tensor_tensor(cq[:, side, :], cq[:, side, :], slr[:, 0, :], ALU.add))
            pool.wait_ge(s_slot, 1)
            pool.wait_ge(s_clear, NT // 4 * DMA)
            for t in range(TT):
                for k in range(K_TOP):
                    g_.indirect_dma_start(out=xsd, out_offset=bass.IndirectOffsetOnAxis(ap=slot_i[:, k, t:t + 1], axis=0),
                                          in_=xn[:, t, :], in_offset=None).then_inc(s_scat, DMA)

            def copy_v(g, par):
                g_.tensor_copy(vg[:, par, :, :, 0:HD],
                               v_sb[:, bass.ds(g, 1), :, :].rearrange("p g t (j d) -> p (g t) j d", d=HD)
                               ).then_inc(s_vg, 1)

            pool.wait_ge(s_free, NJ)
            copy_v(0, 0)
            copy_v(1, 1)
            for u in range(4):
                pool.wait_ge(s_ys[u], NT // 4 * DMA)
            pool.wait_ge(s_sha, TT // 2)

            def gather(n):
                t, k = n // K_TOP, n % K_TOP
                g_.indirect_dma_start(out=yg[:, n % 4, :], out_offset=None, in_=ysd,
                                      in_offset=bass.IndirectOffsetOnAxis(ap=slot_i[:, k, t:t + 1], axis=0)
                                      ).then_inc(s_ga[n % 4], DMA)

            for n in range(3):
                gather(n)
            for n in range(K_TOP * TT):
                if n + 3 < K_TOP * TT:
                    if n >= 1:
                        pool.wait_ge(s_gad, n)
                    gather(n + 3)
                t, k = n // K_TOP, n % K_TOP
                pool.wait_ge(s_ga[n % 4], DMA * (n // 4 + 1))
                g_.tensor_scalar(yg[:, n % 4, :], yg[:, n % 4, :], gates[:, k, t:t + 1], None, ALU.mult
                                 ).then_inc(s_gw, 1)
                pool.wait_ge(s_gw, n + 1)
                if n >= 1:
                    pool.wait_ge(s_gad, n)
                g_.tensor_tensor(x_sb[:, t, :], x_sb[:, t, :], yg[:, n % 4, :], ALU.add).then_inc(s_gad, 1)
            with pool.Fori(0, NG // 2 - 1) as i:
                for par in range(2):
                    pool.wait_ge(s_pv, PV_CREDIT + i * (2 * NS) + NS * (par + 1))
                    copy_v(i * 2 + par + 2, par)

        @block.scalar
        def _(act):
            sc = nc.scalar
            for dst, src in ((ident, c_ident), (cbf, c_bf), (pos_t, c_pos), (coef_t, c_coef), (sel, c_sel)):
                act.dma_start(dst[:, :], src).then_inc(s_c, DMA)
            for half in range(2):
                heads = slopes[half * H // 2:(half + 1) * H // 2].rearrange("(h o) -> h o", o=1)
                act.dma_start(slope_in[:, half:half + 1], heads.unsqueeze(1).broadcast_to([H // 2, N_AUX, 1])
                              ).then_inc(s_c, DMA)
            act.dma_start(qkb_in[:, :], qkv_b[0:2 * D].rearrange("(c p) -> p c", p=P),
                          allow_slow_non_contiguous=True).then_inc(s_c, DMA)
            act.dma_start(vb[:, :], qkv_b[2 * D:3 * D].partition_broadcast(P)).then_inc(s_c, DMA)
            act.dma_start(row[:, :], c_row.partition_broadcast(P)).then_inc(s_c, DMA)
            act.dma_start(eb[:, :], ebias.partition_broadcast(P)).then_inc(s_c, DMA)
            act.wait_ge(s_zero, 2)
            for oc in range(KC):
                for hg in range(H // HG):
                    act.dma_start(wo_nat[:, oc, hg, :, 0:HD],
                                  out_w[oc * P:(oc + 1) * P, hg * HG * HD:(hg + 1) * HG * HD].rearrange(
                                      "p (j d) -> p j d", d=HD)).then_inc(s_wo, DMA)
            act.dma_start(wo_nat[:, :, 0, 0, HD:HD + 1].rearrange("p c o -> p (c o)"),
                          out_b.rearrange("(c p) -> p c", p=P), allow_slow_non_contiguous=True).then_inc(s_wo, DMA)
            act.dma_start(gw[:, :, :], gate_w.rearrange("(c p) e -> p c e", p=P)).then_inc(s_ws, DMA)
            act.dma_start(ws[:, :, 0, :], sg_w.rearrange("(c p) f -> p c f", p=P)).then_inc(s_ws, DMA)
            act.dma_start(ws[:, :, 1, :], su_w.rearrange("(c p) f -> p c f", p=P)).then_inc(s_ws, DMA)
            act.dma_start(wsd[:, :], sd_w).then_inc(s_ws, DMA)
            act.wait_ge(s_c, DMA * N_CONST)
            sc.activation(qkb[:, 0:2], qkb_in[:, 0:2], ACT.Copy, scale=SC).then_inc(s_qkb, 1)
            sc.activation(qkb[:, 2:4], qkb_in[:, 2:4], ACT.Copy).then_inc(s_qkb, 1)
            act.wait_ge(s_qkb, 2)

            def high(n):
                kind, a, b = JOBS[n]
                src = bank(n % 8)
                if kind in ("w", "x", "qk", "r"):
                    act.wait_ge(s_job, n + 1)
                if kind == "w":
                    sc.activation(wh[:, a, b * D:(b + 1) * D], src[:, 0:D], ACT.Copy,
                                  scale=SC if b == 0 else 1.0).then_inc(s_hi, 1)
                elif kind == "x":
                    dst = xh[:, :, 2 * a * P:(2 * a + 2) * P].rearrange("p c (t n) -> p t c n", n=P)
                    sc.activation(dst, src.rearrange("p (t c n) -> p t c n", t=2, c=KC), ACT.Copy).then_inc(s_hi, 1)
                elif kind == "r":
                    sc.activation(prob[:, :, :], src[:, 0:TT * E].rearrange("p (t e) -> p t e", e=E), ACT.Exp,
                                  scale=-1.0).then_inc(s_prob, 1)
                elif kind == "qk":
                    i = QKJ.index(n)
                    if i >= 2:
                        act.wait_ge(s_parts[0][i % 2], 2 * DMA * (i // 2))
                        act.wait_ge(s_res, i - 1)
                    sc.activation(part_h[:, i % 2, :], src, ACT.Identity, bias=qkb[:, a:a + 1]).then_inc(s_hi, 1)
                    if i:
                        middle(i - 1)

            def middle(i):
                act.wait_ge(s_res, i + 1)
                if i >= 2:
                    act.wait_ge(s_parts[1][i % 2], 2 * DMA * (i // 2))
                    act.wait_ge(s_free, QKJ[i - 2] + 1)
                sc.activation(part_m[:, i % 2, :], part_r[:, i % 2, :], ACT.Copy).then_inc(s_mid, 1)

            for n in range(X0):
                high(n)
            act.wait_ge(s_ws, 4 * DMA)
            sc.activation(gwh[:, :, :], gw[:, :, :], ACT.Copy).then_inc(s_small, 1)
            sc.activation(wsh[:, :, :, :], ws[:, :, :, :], ACT.Copy).then_inc(s_small, 1)
            act.wait_ge(s_ln, 2 * TT)
            act.wait_ge(s_zero, 3)
            sc.activation(std[:, :], mv[:, :, 1], ACT.Sqrt, bias=eps_t[:, :]).then_inc(s_std, 1)
            for n in range(X0, NJ):
                high(n)
            middle(NQK - 1)
            for stored in s_parts:
                for i in range(2):
                    act.wait_ge(stored[i], DMA * NQK)
            for c in range(4):
                act.wait_ge(s_g1, c + 1)
                if c >= 2:
                    act.wait_ge(s_h, c - 1)
                sc.activation(th[:, c % 2, :], bank(2 * c), ACT.Tanh, scale=0.5).then_inc(s_th, 1)

            def evacuate_x(k, v):
                act.wait_ge(s_tx, k + 1)
                sc.activation(xt[:, v, :, :], bank(v, KC * P).rearrange("p (c n) -> p c n", c=KC), ACT.Copy
                              ).then_inc(s_xt, 1)

            def tile_tanh(k, v):
                act.wait_ge(s_gu, k + 1)
                sc.activation(te_h[:, v, :], bank(2 + v, F), ACT.Tanh, scale=0.5).then_inc(s_tt, 1)

            def tile_step(k, u, left):
                v = u % 2
                act.wait_ge(s_tht, k + 1)
                sc.activation(ht[:, v, :], bank(4 + v, P), ACT.Copy).then_inc(s_ht, 1)
                if left > 1:
                    tile_tanh(k + 1, 1 - v)
                if left > 2:
                    evacuate_x(k + 2, v)

            evacuate_x(0, 0)
            evacuate_x(1, 1)
            tile_tanh(0, 0)
            with act.Fori(0, NT // 4 - 1) as i:
                for u in range(4):
                    tile_step(i * 4 + u, u, 4)
            for u in range(4):
                tile_step(NT - 4 + u, u, 4 - u)
            sc.activation(std[:, 0:1], std[:, 1:2], ACT.Exp).then_inc(s_exp, EXP_CREDIT)

            def exps(g, s, par):
                qc, kb = STEPS[s]
                lo = max(0, kb * P - qc * CH)
                for j in range(HG):
                    n = HG * s + j
                    act.wait_ge(s_st, g * (HG * NS) + n + 1)
                    if j == 0:
                        act.wait_ge(s_pv, g * NS + s + 1)
                    sc.activation(pt[:, s % 2, j, lo:CH], bank(n % 3)[:, lo:CH], ACT.Exp).then_inc(s_exp, 1)

            def evacuate(g, qc):
                act.wait_ge(s_pv, PV_CREDIT + g * NS + (4 if qc == 0 else NS))
                sc.activation(ot[:, bass.ds(g, 1), qc * CH:(qc + 1) * CH].rearrange("p g s -> p (g s)"),
                              bank(OUT_BANK), ACT.Copy).then_inc(s_ev, 1)

            def pair(g):
                for s in range(2 * NS):
                    par, st = s // NS, s % NS
                    exps(g + par, st, par)
                    if st == 4:
                        evacuate(g + par, 0)
                    if s == NS:
                        evacuate(g, 1)
                evacuate(g + 1, 1)

            with act.Fori(0, NG // 2 - 1) as i:
                pair(i * 2)
            pair(NG - 2)
            act.wait_ge(s_rden, 1)
            for g in range(NG):
                r = slice(g * QT, (g + 1) * QT)
                sc.activation(rden_x[:, r, :, :], rden[:, r, :].unsqueeze(3).broadcast_to([P, QT, HG, 32]), ACT.Copy
                              ).then_inc(s_rx, 1)

        @block.vector
        def _(dve):
            v = nc.vector
            v.memset(mx[:, :, :], 0.0).then_inc(s_mxf, MX_CREDIT)
            for t in range(TT):
                if t % 4 == 0:
                    dve.wait_ge(s_x[t // 4], DMA)
                v.bn_stats(stats[:, t, :], x_sb[:, t, :]).then_inc(s_ln, 1)
            for t in range(TT):
                dve.wait_ge(s_ln, t + 1)
                v.bn_aggr(mv[:, t, :], stats[:, t, :]).then_inc(s_ln, 1)
            dve.wait_ge(s_pool, 2 + 5 + 10)
            for n in range(4):
                side, half = n // 2, n % 2
                v.tensor_scalar(aux[:, n, :], pos_t[:, side * S:(side + 1) * S], cq[:, side, half:half + 1], None,
                                ALU.mult).then_inc(s_aux, 1)

            def low(n):
                kind, a, b = JOBS[n]
                dve.wait_ge(s_job, n + 1)
                src = bank(n % 8)
                if kind == "w":
                    dve.wait_ge(s_hi, HI_OF[n])
                    v.scalar_tensor_tensor(wl[:, a, b * D:(b + 1) * D], src[:, 0:D], SC if b == 0 else 1.0,
                                           wh[:, a, b * D:(b + 1) * D], ALU.mult, ALU.subtract).then_inc(s_free, 1)
                elif kind == "o":
                    v.tensor_copy(wo_t[:, :, a * P:(a + 1) * P],
                                  src.rearrange("p (g n) -> p g n", n=P)).then_inc(s_free, 1)
                elif kind == "x":
                    dve.wait_ge(s_hi, HI_OF[n])
                    cols = slice(2 * a * P, (2 * a + 2) * P)
                    v.tensor_tensor(xl[:, :, cols].rearrange("p c (t n) -> p t c n", n=P),
                                    src.rearrange("p (t c n) -> p t c n", t=2, c=KC),
                                    xh[:, :, cols].rearrange("p c (t n) -> p t c n", n=P),
                                    ALU.subtract).then_inc(s_free, 1)
                elif kind == "r":
                    route()
                elif kind == "k":
                    place()
                elif kind == "qk":
                    i = QKJ.index(n)
                    dve.wait_ge(s_hi, HI_OF[n])
                    v.scalar_tensor_tensor(part_r[:, i % 2, :], src, qkb[:, a:a + 1], part_h[:, i % 2, :],
                                           ALU.add, ALU.subtract).then_inc(s_res, 1)
                    dve.wait_ge(s_mid, i + 1)
                    if i >= 2:
                        dve.wait_ge(s_parts[2][i % 2], 2 * DMA * (i // 2))
                    v.tensor_tensor(part_l[:, i % 2, :], part_r[:, i % 2, :], part_m[:, i % 2, :],
                                    ALU.subtract).then_inc(s_free, 1)
                else:
                    t = 2 * a
                    b_, kb = t // QT, t % QT
                    dst = v_sb[:, 4 * b_:4 * b_ + 4, kb:kb + 2, :].rearrange("p g t n -> p t g n")
                    v.tensor_tensor(dst, src.rearrange("p (t g n) -> p t g n", t=2, g=4),
                                    vb[:, :].rearrange("p (o g n) -> p o g n", o=1, g=4).to_broadcast([P, 2, 4, HG * HD]),
                                    ALU.add).then_inc(s_free, 1)

            steps = [0]

            def then(ins):
                ins.then_inc(s_r, 1)
                steps[0] += 1
                dve.wait_ge(s_r, steps[0])

            def over_e(ap):
                return ap.unsqueeze(2).broadcast_to([P, TT, E])

            def over_t(ap):
                return ap.unsqueeze(1).broadcast_to([P, TT, E])

            rank_row = row[:, 0:E]
            before = row[:, E:E + E * E].rearrange("p (a b) -> p a b", b=E)
            fills = row[:, E + E * E:E + 2 * E * E].rearrange("p (a b) -> p a b", b=E)
            tile_no = row[:, E + 2 * E * E:].rearrange("p (k e) -> p k e", e=E)

            def route():
                dve.wait_ge(s_prob, 1)
                then(v.tensor_scalar(rt[:, :, :], prob[:, :, :], 1.0, None, ALU.add))
                then(v.reciprocal(prob[:, :, :], rt[:, :, :]))
                then(v.tensor_tensor(biased[:, :, :], prob[:, :, :], over_t(eb[:, :]), ALU.add))
                for k in range(K_TOP):
                    p_ = pick[:, k, :, :]
                    then(v.reduce_max(top[:, 0, :], biased[:, :, :], axis=AX.X))
                    then(v.tensor_tensor(rt[:, :, :], biased[:, :, :], over_e(top[:, 0, :]), ALU.is_equal))
                    then(v.tensor_tensor(rt[:, :, :], rt[:, :, :], over_t(rank_row), ALU.mult))
                    then(v.reduce_max(top[:, 1, :], rt[:, :, :], axis=AX.X))
                    then(v.tensor_tensor(p_, rt[:, :, :], over_e(top[:, 1, :]), ALU.is_equal))
                    if k == 0:
                        then(v.scalar_tensor_tensor(biased[:, :, :], p_, NEG, biased[:, :, :], ALU.mult, ALU.add))
                v.tensor_tensor(picked[:, :, :], pick[:, 0, :, :], pick[:, 1, :, :], ALU.add).then_inc(s_picked, 1)
                for k in range(K_TOP):
                    then(v.tensor_tensor(rt[:, :, :], pick[:, k, :, :], prob[:, :, :], ALU.mult))
                    then(v.reduce_sum(top[:, 2 + k, :], rt[:, :, :], axis=AX.X))
                then(v.scalar_tensor_tensor(top[:, 4, :], top[:, 2, :], 1e-20, top[:, 3, :], ALU.add, ALU.add))
                then(v.reciprocal(top[:, 5, :], top[:, 4, :]))
                for k in range(K_TOP):
                    then(v.tensor_tensor(gates[:, k, :], top[:, 2 + k, :], top[:, 5, :], ALU.mult))
                v.memset(mv_pad[:, 3:4], 0.0).then_inc(s_free, 1)

            def place():
                ranks = bank(JOBS.index(("k", 0, 0)) % 8)
                counts = ranks[:, TT * E:TT * E + E]
                sq = [P, E, E]
                then(v.tensor_tensor(rt[:, :, :], counts.unsqueeze(2).broadcast_to(sq), fills, ALU.is_gt))
                then(v.reduce_sum(cnt[:, 0, :], rt[:, :, :], axis=AX.X))
                then(v.tensor_tensor(rt[:, :, :], cnt[:, 0, :].unsqueeze(1).broadcast_to(sq), before, ALU.mult))
                then(v.reduce_sum(cnt[:, 1, :], rt[:, :, :], axis=AX.X))
                then(v.tensor_tensor(cnt[:, 2, :], cnt[:, 0, :], cnt[:, 1, :], ALU.add))
                then(v.tensor_scalar(cnt[:, 3, :], cnt[:, 1, :], float(P), None, ALU.mult))
                then(v.tensor_tensor(rt[:, :, :], ranks[:, 0:TT * E].rearrange("p (t e) -> p t e", e=E),
                                     over_t(cnt[:, 3, :]), ALU.add))
                for k in range(K_TOP):
                    then(v.tensor_tensor(biased[:, :, :], pick[:, k, :, :], rt[:, :, :], ALU.mult))
                    then(v.reduce_sum(slot_f[:, k, :], biased[:, :, :], axis=AX.X))
                v.tensor_copy(slot_i[:, :, :], slot_f[:, :, :]).then_inc(s_slot, 1)
                et = etab[:, :].rearrange("p (k e) -> p k e", e=E)
                then(v.tensor_tensor(et, cnt[:, 2, :].unsqueeze(1).broadcast_to([P, NT, E]), tile_no, ALU.is_le))
                then(v.reduce_sum(eid_f[:, :], et, axis=AX.X))
                v.tensor_scalar(eid[:, :], eid_f[:, :], float(E - 1), None, ALU.min).then_inc(s_free, 1)

            for n in range(X0):
                low(n)
            dve.wait_ge(s_small, 2)
            v.tensor_tensor(gwl[:, :, :], gw[:, :, :], gwh[:, :, :], ALU.subtract).then_inc(s_smalll, 1)
            v.tensor_tensor(wsl[:, :, :, :], ws[:, :, :, :], wsh[:, :, :, :], ALU.subtract).then_inc(s_smalll, 1)
            dve.wait_ge(s_std, 1)
            v.reciprocal(rstd[:, :], std[:, :]).then_inc(s_ln, 1)
            dve.wait_ge(s_ln, 2 * TT + 1)
            for t in range(TT):
                v.tensor_scalar(xn[:, t, :], x_sb[:, t, :], mv[:, t, 0:1], rstd[:, t:t + 1],
                                ALU.subtract, ALU.mult).then_inc(s_xn, 1)
            for n in range(X0, NJ):
                low(n)
            for c in range(4):
                dve.wait_ge(s_th, c + 1)
                v.scalar_tensor_tensor(th[:, c % 2, :], th[:, c % 2, :], 1.0, bank(2 * c), ALU.add, ALU.mult
                                       ).then_inc(s_ta, 1)
                dve.wait_ge(s_ta, c + 1)
                if c >= 2:
                    dve.wait_ge(s_sh, 2 * (c - 1))
                v.scalar_tensor_tensor(hsh[:, c % 2, :], th[:, c % 2, :], 0.5, bank(2 * c + 1), ALU.mult, ALU.mult
                                       ).then_inc(s_h, 1)
            for n in range(TT // 2):
                dve.wait_ge(s_sh, n + 1)
                xs = x_sb[:, 2 * n:2 * n + 2, :].rearrange("p t d -> p (t d)")
                v.tensor_tensor(xs, xs, bank(n), ALU.add).then_inc(s_sha, 1)

            def tile_hidden(k, w):
                dve.wait_ge(s_tt, k + 1)
                v.scalar_tensor_tensor(te_h[:, w, :], te_h[:, w, :], 1.0, bank(2 + w, F), ALU.add, ALU.mult
                                       ).then_inc(s_tstep, 1)
                dve.wait_ge(s_tstep, k + 1)
                v.scalar_tensor_tensor(hh[:, w, :], te_h[:, w, :], 0.5, ps[:, (2 + w) * CH + F:(2 + w) * CH + 2 * F],
                                       ALU.mult, ALU.mult).then_inc(s_hh, 1)

            def tile_step(k, u, left, stored):
                if left > 1:
                    tile_hidden(k + 1, (u + 1) % 2)
                dve.wait_ge(s_dn, k + 1)
                if stored is not None:
                    dve.wait_ge(s_ys[u], stored)
                v.tensor_copy(y_out[:, u, :], bank(6 + u % 2, D)).then_inc(s_yo, 1)

            tile_hidden(0, 0)
            for u in range(4):
                tile_step(u, u, 4, None)
            with dve.Fori(1, NT // 4 - 1) as i:
                for u in range(4):
                    tile_step(i * 4 + u, u, 4, i * DMA)
            for u in range(4):
                tile_step(NT - 4 + u, u, 4 - u, (NT // 4 - 1) * DMA)

            def maxima(g, par, p):
                n = g * NP + p
                qt, j0, nj = PIECES[p]
                w = (qt + 1) * P
                dve.wait_ge(s_mxr, n + 1)
                src = ps[:, (4 + 2 * (p % 2)) * CH:(4 + 2 * (p % 2)) * CH + nj * w].rearrange("p (j w) -> p j w", j=nj)
                dst = mx[:, par, :].rearrange("p (j t) -> p j t", j=HG)[:, j0:j0 + nj, qt]
                last = v.reduce_max(dst, src, axis=AX.X)
                last.then_inc(s_mxf, 1)

            def negate(g, par):
                dve.wait_ge(s_mxr, (g + 1) * NP)
                src = bank(6, P, HG * QT)
                v.tensor_scalar(nr[:, par, 0, :], src, -1.0, None, ALU.mult).then_inc(s_nstep, 1)
                dve.wait_ge(s_nstep, g * 2 + 1)
                v.scalar_tensor_tensor(nrf[:, par, :], src, -1.0, nr[:, par, 0, :], ALU.mult,
                                       ALU.subtract).then_inc(s_mxf, 1)
                dve.wait_ge(s_mxf, MX_CREDIT + (g + 1) * NP)
                v.tensor_copy(nr[:, par, 1, :], nrf[:, par, :]).then_inc(s_nstep, 1)
                dve.wait_ge(s_nstep, g * 2 + 2)
                v.tensor_tensor(nr[:, par, 2, :], nrf[:, par, :], nr[:, par, 1, :], ALU.subtract).then_inc(s_n, 1)

            def beside(g, par, ahead):
                for dg, p in [x[1:] for x in ORDER if x[0] == "max"]:
                    if dg > ahead:
                        continue
                    q = (par + dg) % 2
                    if p == NP - 1:
                        negate(g + dg, q)
                    else:
                        maxima(g + dg, q, p)

            for p in range(NP - 1):
                maxima(0, 0, p)
            negate(0, 0)
            for p in range(EARLY):
                maxima(1, 1, p)

            with dve.Fori(0, NG // 2 - 1) as i:
                for par in range(2):
                    beside(i * 2 + par, par, 2)
            beside(NG - 2, 0, 1)
            dve.wait_ge(s_sum, 1)
            v.reciprocal(rden[:, :, :], bank(4, NG * QT * HG).rearrange("p (n j) -> p n j", j=HG)).then_inc(s_rden, 1)
            dve.wait_ge(s_gad, K_TOP * TT)
            for b in range(B):
                for n in range(NG * b, NG * (b + 1)):
                    g, qc = n // 2, n % 2
                    dve.wait_ge(s_bc, n + 1)
                    o = ot[:, g, qc * CH:(qc + 1) * CH]
                    v.tensor_tensor(o, o, bank(n % 4), ALU.mult).then_inc(s_dv, 1)
                for t in range(b * QT, (b + 1) * QT):
                    dve.wait_ge(s_pr, t + 1)
                    v.tensor_tensor(x_sb[:, t, :], x_sb[:, t, :], bank(4 + t % 4, D), ALU.add).then_inc(s_add, 1)

        @block.tensor
        def _(pe):
            te = nc.tensor

            def split_product(out, sides, first=True, last=True):
                ops = [(l, r) for (ah, al, bh, bl) in sides for l, r in ((al, bh), (ah, bl), (ah, bh))]
                for k, (l, r) in enumerate(ops):
                    ins = te.matmul(out, l, r, start=k == 0, stop=k == len(ops) - 1)
                return ins

            pe.wait_ge(s_c, DMA * N_CONST)
            for n, (kind, a, b) in enumerate(JOBS):
                out = bank(n % 8)
                if n >= 8:
                    pe.wait_ge(s_free, n - 7)
                if kind == "w":
                    pe.wait_ge(s_w, DMA)
                    for k in range(2):
                        ins = te.transpose(out[:, k * P:(k + 1) * P], w_nat[:, 2 * b + k, a * P:(a + 1) * P], ident[:, :])
                elif kind == "o":
                    pe.wait_ge(s_wo, 9 * DMA)
                    for hg in range(H // HG):
                        ins = te.transpose(out[:, hg * P:(hg + 1) * P],
                                           wo_nat[:, a, hg, :, :].rearrange("p j d -> p (j d)"), ident[:, :])
                elif kind == "x":
                    pe.wait_ge(s_xn, 2 * a + 2)
                    for k in range(4):
                        ins = te.transpose(out[:, k * P:(k + 1) * P],
                                           xn[:, 2 * a + k // 2, k % 2 * P:(k % 2 + 1) * P], ident[:, :])
                elif kind == "r":
                    pe.wait_ge(s_free, R0)
                    pe.wait_ge(s_smalll, 2)
                    for t in range(TT):
                        ts = slice(t * P, (t + 1) * P)
                        ops = [(l, r) for c in range(KC)
                               for l, r in ((xl[:, c, ts], gwl[:, c, :]), (xl[:, c, ts], gwh[:, c, :]),
                                            (xh[:, c, ts], gwl[:, c, :]), (xh[:, c, ts], gwh[:, c, :]))]
                        for k, (l, r) in enumerate(ops):
                            ins = te.matmul(out[:, t * E:(t + 1) * E], l, r, start=k == 0, stop=k == len(ops) - 1)
                elif kind == "k":
                    pe.wait_ge(s_picked, 1)
                    for t in range(TT):
                        te.matmul(out[:, TT * E:TT * E + E], cbf[:, 4 * P:5 * P], picked[:, t, :],
                                  start=t == 0, stop=t == TT - 1)
                    te.matmul(out[:, 0:TT * E], cbf[:, 3 * P:4 * P], picked[:, :, :].rearrange("p t e -> p (t e)"),
                              start=True, stop=False)
                    for t in range(TT - 1):
                        ins = te.matmul(out[:, (t + 1) * E:TT * E], cbf[:, 4 * P:5 * P],
                                        picked[:, t, :].unsqueeze(1).broadcast_to([P, TT - 1 - t, E]),
                                        start=False, stop=t == TT - 2)
                elif kind == "qk":
                    f, t = slice(a * P, (a + 1) * P), slice(b * CH, (b + 1) * CH)
                    ins = split_product(out, [(wh[:, c, f], wl[:, c, f], xh[:, c, t], xl[:, c, t]) for c in range(KC)])
                else:
                    w = slice(2 * D, 3 * D)
                    for k in range(2):
                        t = slice((2 * a + k) * P, (2 * a + k + 1) * P)
                        ins = split_product(out[:, k * D:(k + 1) * D],
                                            [(xh[:, c, t], xl[:, c, t], wh[:, c, w], wl[:, c, w]) for c in range(KC)])
                ins.then_inc(s_job, 1)

            def shared_down(c):
                pe.wait_ge(s_h, c + 1)
                for t in range(4):
                    ins = te.matmul(ps[:, 2 * c * CH + t * D:2 * c * CH + (t + 1) * D],
                                    hsh[:, c % 2, t * P:(t + 1) * P], wsd[:, :], start=True, stop=True)
                    if t % 2:
                        ins.then_inc(s_sh, 1)

            pe.wait_ge(s_free, NJ)
            for c in range(4):
                t = slice(c * CH, (c + 1) * CH)
                for k in range(2):
                    ins = split_product(bank(2 * c + k), [(wsh[:, m, k, :], wsl[:, m, k, :], xh[:, m, t], xl[:, m, t])
                                                          for m in range(KC)])
                ins.then_inc(s_g1, 1)
                if c:
                    shared_down(c - 1)
            shared_down(3)

            def tile_in(k, u, need):
                pe.wait_ge(s_xin[u], need)
                for c in range(KC):
                    ins = te.transpose(ps[:, (u % 2) * CH + c * P:(u % 2) * CH + (c + 1) * P],
                                       x_in[:, u, c * P:(c + 1) * P], ident[:, :])
                ins.then_inc(s_tx, 1)

            def expert_of(k):
                return pe.value_load(eid[0:1, bass.ds(k, 1)], min_val=0, max_val=E - 1)

            def gate_up(k, w):
                e = expert_of(k)
                pe.wait_ge(s_xt, k + 1)
                for c in range(KC):
                    ins = te.matmul(bank(2 + w, 2 * F), xt[:, w, c, :],
                                    w_gu[:, bass.ds(e, 1), c, :].rearrange("p o f -> p (o f)"),
                                    start=c == 0, stop=c == KC - 1)
                ins.then_inc(s_gu, 1)

            def tile_step(k, u, left, need):
                w = u % 2
                pe.wait_ge(s_hh, k + 1)
                te.transpose(bank(4 + w, P), hh[:, w, :], ident[:, :]).then_inc(s_tht, 1)
                if left > 1:
                    gate_up(k + 1, 1 - w)
                if left > 2:
                    tile_in(k + 2, (u + 2) % 4, need)
                e = expert_of(k)
                pe.wait_ge(s_ht, k + 1)
                te.matmul(bank(6 + w, D), ht[:, w, :], w_dn[:, bass.ds(e, 1), :].rearrange("p o f -> p (o f)"),
                          start=True, stop=True).then_inc(s_dn, 1)

            pe.wait_ge(s_sha, TT // 2)
            tile_in(0, 0, DMA)
            tile_in(1, 1, DMA)
            pe.wait_ge(s_wgu, DMA)
            pe.wait_ge(s_wdn, DMA)
            gate_up(0, 0)
            with pe.Fori(0, NT // 4 - 1) as i:
                for u in range(4):
                    tile_step(i * 4 + u, u, 4, (i + (u + 2) // 4 + 1) * DMA)
            for u in range(4):
                tile_step(NT - 4 + u, u, 4 - u, NT // 4 * DMA)
            pe.wait_ge(s_yo, NT)

            def max_scores(g, par, p):
                pe.wait_ge(s_mxf, g * NP + p + 1)
                base = (4 + 2 * (p % 2)) * CH
                if p == NP - 1:
                    pe.wait_ge(s_mxf, MX_CREDIT + g * NP + NP - 1)
                    te.transpose(bank(6, P, HG * QT), mx[:, par, :], ident[:, :]).then_inc(s_mxr, 1)
                    return
                qt, j0, nj = PIECES[p]
                w = (qt + 1) * P
                for j in range(j0, j0 + nj):
                    at = base + (j - j0) * w
                    q = qs[0:K_MAX, par, j, qt * P:(qt + 1) * P]
                    for c in range(0, w, CH):
                        e = min(w, c + CH)
                        te.matmul(ps[:, at + c:at + e], q, ks[0:K_MAX, par, j, c:e], start=True, stop=e < w)
                    ins = te.matmul(ps[:, at + w - P:at + w], idb, mask_q, start=False, stop=True)
                ins.then_inc(s_mxr, 1)

            def exp_scores(g, s, par, heads):
                qc, kb = STEPS[s]
                lo = max(0, kb * P - qc * CH)
                diag = kb * P >= qc * CH
                for j in heads:
                    n = HG * s + j
                    pe.wait_ge(s_exp, g * (HG * NS) + n + 1)
                    out = bank(n % 3)
                    ins = te.matmul(out[:, lo:CH], ks[0:K_EXP, par, j, kb * P:(kb + 1) * P],
                                    qs[0:K_EXP, par, j, qc * CH + lo:(qc + 1) * CH], start=True, stop=not diag)
                    if diag:
                        ins = te.matmul(out[:, lo:lo + P], idb, mask_k, start=False, stop=True)
                    ins.then_inc(s_st, 1)

            def weigh(g, s, par):
                qc, kb = STEPS[s]
                lo = max(0, kb * P - qc * CH)
                pe.wait_ge(s_exp, EXP_CREDIT + g * (HG * NS) + HG * (s + 1))
                if kb == 0:
                    pe.wait_ge(s_ev, g * 2 + qc + 1)
                for j in range(HG):
                    ins = te.matmul(ps[32 * j:32 * j + 32, OUT_BANK * CH + lo:(OUT_BANK + 1) * CH], vg[:, par, kb, j, :],
                                    pt[:, s % 2, j, lo:CH], start=kb == 0, stop=kb == 4 * qc + 3,
                                    tile_position=(0, 32 * j))
                ins.then_inc(s_pv, 1)


            def pair(g, last, count):
                for par in range(2):
                    pe.wait_ge(s_nl[par], count * (3 * DMA))
                    pe.wait_ge(s_vg, g + par + 1)
                    for kind, a, b in [(*x, 0)[:3] for x in ORDER]:
                        if kind == "exp":
                            exp_scores(g + par, a, par, [b])
                        elif kind == "out" and a + par:
                            weigh(g + par - (a == 0), (a - 1) % NS, par - (a == 0))
                        elif kind == "max" and not (last and a + par > 1):
                            q = (par + a) % 2
                            if b in (0, 11):
                                for side in range(2):
                                    pe.wait_ge(s_ld[side][int(b > 0)][q], (count + (par + a) // 2) * (LOADS * DMA))
                            max_scores(g + par + a, q, b)
                weigh(g + 1, NS - 1, 1)

            for g, n in ((0, NP), (1, EARLY)):
                for p in range(n):
                    if p in (0, 11):
                        for side in range(2):
                            pe.wait_ge(s_ld[side][int(p > 0)][g], LOADS * DMA)
                    max_scores(g, g, p)
            with pe.Fori(0, NG // 2 - 1) as i:
                pair(i * 2, False, i + 1)
            pair(NG - 2, True, NG // 2)

            pe.wait_ge(s_ev, 1 + 2 * NG)
            sums = bank(4, NG * QT * HG).rearrange("p (n j) -> p n j", j=HG)
            for n in range(NG * QT):
                g, qt = n // QT, n % QT
                ins = te.matmul(sums[:, n, :], ot[:, g, qt * P:(qt + 1) * P], sel[:, 0:P:32], start=True, stop=True)
            ins.then_inc(s_sum, 1)
            for b in range(B):
                for n in range(NG * b, NG * (b + 1)):
                    if n >= 4:
                        pe.wait_ge(s_dv, n - 3)
                    pe.wait_ge(s_rx, n // 2 + 1)
                    for k in range(4):
                        ins = te.matmul(bank(n % 4)[:, k * P:(k + 1) * P],
                                        rden_x[:, 4 * n + k, :, :].rearrange("p j m -> p (j m)"), ident[:, :],
                                        start=True, stop=True)
                    ins.then_inc(s_bc, 1)
                for t in range(b * QT, (b + 1) * QT):
                    pe.wait_ge(s_dv, NG * (b + 1))
                    if t >= 4:
                        pe.wait_ge(s_add, t - 3)
                    for hg in range(H // HG):
                        ins = te.matmul(bank(4 + t % 4, D), ot[:, b * 4 + hg, t % QT * P:(t % QT + 1) * P],
                                        wo_t[:, hg, :], start=hg == 0, stop=hg == 3)
                    ins.then_inc(s_pr, 1)


NAMES = {
    "L0_attn_hidden_states": "x", "L0_attn_qkv_w": "qkv_w", "L0_attn_qkv_b": "qkv_b", "L0_attn_out_w": "out_w",
    "L0_attn_out_b": "out_b", "L0_attn_alibi_slopes": "slopes", "L0_ffn_gate_w": "gate_w",
    "L0_ffn_expert_bias": "ebias", "L0_ffn_shared_gate_w": "sg_w", "L0_ffn_shared_up_w": "su_w",
    "L0_ffn_shared_down_w": "sd_w", "L0_ffn_experts_gate_up": "e_gu", "L0_ffn_experts_down": "e_dn",
}


def kernel(**inputs):
    import concourse.bacc as bacc
    from concourse.bass_utils import run_bass_kernel_spmd

    nc = bacc.Bacc("TRN2", target_bir_lowering=False, num_devices=1)
    arrays = {short: np.ascontiguousarray(inputs[name]) for name, short in NAMES.items()}
    arrays.update(constants())
    args = [nc.dram_tensor(k, a.shape, mybir.dt.from_np(a.dtype), kind="ExternalInput").ap()
            for k, a in arrays.items()]
    out = nc.dram_tensor("y", (B, S, D), F32, kind="ExternalOutput").ap()
    build(nc, *args, out)
    return run_bass_kernel_spmd(nc, [arrays], core_ids=[0]).results[0]["y"]
```

```python
from contextlib import ExitStack

import numpy as np

import concourse.bass as bass
import concourse.mybir as mybir

F32 = mybir.dt.float32
F32R = mybir.dt.float32r
BF16 = mybir.dt.bfloat16
I32 = mybir.dt.int32
ALU = mybir.AluOpType
ACT = mybir.ActivationFunctionType
AX = mybir.AxisListType

P = 128
B, S, D, H = 2, 1024, 256, 16
HD = D // H
T = B * S
TT = T // P
KC = D // P
E, F, K_TOP = 16, 128, 2
NT = (K_TOP * T + E * (P - 1)) // P + 1
NT = -(-NT // 4) * 4
SLOTS = NT * P
HG = 4
NG = B * H // HG
QT = S // P
CH = 512
NEG = -1.0e30
LN_EPS = 1e-5

Q_PARTS = (0, 0, 0, 1, 1, 2)
K_PARTS = (0, 1, 2, 0, 1, 0)
AUX0 = 6 * HD
N_ALIBI = 12
N0 = AUX0 + N_ALIBI
K_MAX = N0
K_EXP = N0 + 3
N_AUX = K_EXP - AUX0
AUXP = H // 2 * N_AUX

STEPS = [(qc, kb) for qc in range(2) for kb in range(4 * qc + 4)]
NS = len(STEPS)


def max_pieces():
    out = [(0, 0, 4), (1, 0, 2), (1, 2, 2)]
    for qt in range(2, QT):
        out += [(qt, j, 1) for j in range(HG)]
    return out


PIECES = max_pieces()
NP = len(PIECES) + 1
RING = 4
EARLY = 7


def schedule():
    items = [("exp", s, j) for s in range(NS) for j in range(HG)]
    exp_cost = [CH - max(0, STEPS[s][1] * P - STEPS[s][0] * CH) + 230 for _, s, _ in items]
    pieces = []
    for (ahead, ps), (start, end) in WINDOWS:
        cost = [(1 + PIECES[p][0]) * P * PIECES[p][2] + 200 if p < NP - 1 else 100 for p in ps]
        pieces += [(start + (end - start) * sum(cost[:n]) / sum(cost), ahead, p) for n, p in enumerate(ps)]
    pieces.sort()
    out, now = [], 0
    for item, cost in zip(items, exp_cost):
        out.append(item)
        if item[2] == OUT_AFTER:
            out.append(("out", item[1]))
        now += cost / sum(exp_cost)
        while pieces and pieces[0][0] <= now:
            out.append(("max", *pieces.pop(0)[1:]))
    return out + [("max", *x[1:]) for x in pieces]


FIRST_HALF = 11
WINDOWS = [((1, range(EARLY, FIRST_HALF)), (0.0, 0.17)), ((1, range(FIRST_HALF, NP)), (0.17, 0.84)),
           ((2, range(EARLY)), (0.85, 1.0))]
OUT_AFTER = 2
ORDER = schedule()

FINAL = ([("divide", n) for n in range(2 * NG - 2)] + [("project", t) for t in range(QT)]
         + [("divide", n) for n in range(2 * NG - 2, 2 * NG)] + [("project", t) for t in range(QT, B * QT)])
BESIDE = 2 * NG - 2 + 3
SUMS_AT = BESIDE + 1


def constants():
    bf = mybir.dt.np(BF16)
    k = np.arange(P)
    above = np.where(k[None, :] > k[:, None], NEG, 0.0)
    pos = np.arange(S)
    a, b, one = pos // 8 * 8, pos % 8, np.ones(S)
    tq = np.stack([one, a, one, b] * 3 + [one] * 3)
    tk = np.stack([a, one, b, one] * 3 + [one] * 3)
    coef = np.zeros((N_AUX, 2, 4), np.float32)
    for r in range(N_ALIBI):
        if r % 2 == 0:
            coef[r, 0, r // 4] = 1
            coef[r, 1, 3] = 1
        else:
            coef[r, 0, 3] = 1
            coef[r, 1, r // 4] = -1
    coef[N_ALIBI:, 1, 3] = 1
    e = np.arange(E)
    row = np.concatenate([E - e, (e[None, :] < e[:, None]).ravel(), np.tile(P * e, E), np.repeat(np.arange(NT), E)])
    sel = (np.arange(P)[None, :] // 32 == np.arange(HG)[:, None]).astype(np.float32)
    perm = np.zeros((P, P), np.float32)
    perm[k, k // (P // 2) * (P // 2) + k % HD * HG + k // HD % HG] = 1
    lower = (k[:, None] < k[None, :]).astype(np.float32)
    return {
        "c_ident": np.eye(P, dtype=np.float32),
        "c_perm": perm,
        "c_bf": np.concatenate([np.eye(P), above, above.T, lower, np.ones((P, P))], 1).astype(bf),
        "c_pos": np.tile(np.concatenate([tq, tk], 1), (H // 2, 1)).astype(bf),
        "c_coef": np.tile(coef.reshape(N_AUX, 8), (H // 2, 1)),
        "c_sel": sel,
        "c_row": row.astype(np.float32),
    }


def build(nc, x, qkv_w, qkv_b, out_w, out_b, slopes, gate_w, ebias, sg_w, su_w, sd_w, e_gu, e_dn,
          c_ident, c_perm, c_bf, c_pos, c_coef, c_sel, c_row, y):
    ctx = ExitStack()
    with ctx:
        def sb(name, shape, dt=F32):
            return ctx.enter_context(nc.sbuf_tensor(name, shape, dt))

        def sem(name):
            return ctx.enter_context(nc.semaphore(name))

        x_sb = sb("x_sb", [P, TT, D])
        wo_t = sb("wo_t", [P, H // HG, D])
        ident = sb("ident", [P, P])
        cbf = sb("cbf", [P, 5 * P], BF16)
        sel = sb("sel", [HG, P])
        v_sb = sb("v_sb", [P, NG, QT, HG * HD])
        yg = sb("yg", [P, 4, D])
        mx = sb("mx", [P, 2, HG * QT])
        nr = sb("nr", [HG * QT, 2, 3, P], BF16)
        nrf = sb("nrf", [HG * QT, 2, P])
        slot_i = sb("slot_i", [P, K_TOP, TT], I32)
        eid = sb("eid", [P, NT], I32)
        gates = sb("gates", [P, K_TOP, TT])
        mv_pad = sb("mv_pad", [P, 12])
        vg = sb("vg", [P, 2, QT, HG, 32])
        ps = ctx.enter_context(nc.psum_tensor("ps", [P, 8 * CH], F32))

        with nc.sbuf_tensor("xh", [P, KC, T], F32R) as xh, nc.sbuf_tensor("xl", [P, KC, T], F32R) as xl:
            pass
        qs = sb("qs", [P, 2, HG, S], BF16)
        ks = sb("ks", [P, 2, HG, S], BF16)
        with ExitStack() as early:
            def tmp(name, shape, dt=F32):
                return early.enter_context(nc.sbuf_tensor(name, shape, dt))

            xn = tmp("xn", [P, TT, D])
            with ExitStack() as first:
                parts = first.enter_context(nc.sbuf_tensor("parts", [P, RING, 3, CH], BF16))
                part_r = first.enter_context(nc.sbuf_tensor("part_r", [P, RING, CH], F32))
            w_gu = tmp("w_gu", [P, E, KC, 2 * F])
            wh = tmp("wh", [P, KC, 3 * D], F32R)
            wl = tmp("wl", [P, KC, 3 * D], F32R)
            gw = tmp("gw", [P, KC, E])
            gwh = tmp("gwh", [P, KC, E], F32R)
            gwl = tmp("gwl", [P, KC, E], F32R)
            ws = tmp("ws", [P, KC, 2, F])
            wsh = tmp("wsh", [P, KC, 2, F], F32R)
            wsl = tmp("wsl", [P, KC, 2, F], F32R)
            wsd = tmp("wsd", [P, D])
            perm = tmp("perm", [P, P])
            qkb = tmp("qkb", [P, 4])
            qkb_in = tmp("qkb_in", [4, P])
            qkb_row = tmp("qkb_row", [4, P])
            vb = tmp("vb", [P, D])
            eb = tmp("eb", [P, E])
            row = tmp("row", [P, E + 2 * E * E + NT * E])
            eps_t = tmp("eps_t", [P, 1])
            stats = tmp("stats", [P, TT, 6])
            mv = tmp("mv", [P, TT, 2])
            std = tmp("std", [P, TT])
            rstd = tmp("rstd", [P, TT])
            coef_t = tmp("coef_t", [AUXP, 8])
            slope_in = tmp("slope_in", [AUXP, 2])
            sl = tmp("sl", [AUXP, 3, 2], BF16)
            slr = tmp("slr", [AUXP, 3, 2])
            cq = tmp("cq", [AUXP, 2, 2])
            prob = tmp("prob", [P, TT, E])
            biased = tmp("biased", [P, TT, E])
            rt = tmp("rt", [P, TT, E])
            pick = tmp("pick", [P, K_TOP, TT, E])
            picked = tmp("picked", [P, TT, E], BF16)
            top = tmp("top", [P, 8, TT])
            cnt = tmp("cnt", [P, 4, E])
            etab = tmp("etab", [P, NT * E])
            slot_f = tmp("slot_f", [P, K_TOP, TT])
            eid_f = tmp("eid_f", [P, NT])
            y_out = tmp("y_out", [P, 4, D])
            ht = tmp("ht", [P, 2, P])
            with ExitStack() as first:
                te_h = first.enter_context(nc.sbuf_tensor("te_h", [P, 2, F], F32))
                hh = first.enter_context(nc.sbuf_tensor("hh", [P, 2, F], F32))
            with nc.sbuf_tensor("logits_t", [E, T], F32) as logits_t:
                pass
            th = tmp("th", [P, 2, CH])
            hsh = tmp("hsh", [P, 2, CH])
            with ExitStack() as first:
                def now(name, shape, dt=F32):
                    return first.enter_context(nc.sbuf_tensor(name, shape, dt))

                w_nat = now("w_nat", [P, 6, D])
                wo_nat = now("wo_nat", [P, KC, H // HG, HG, 32])
                pos_t = now("pos_t", [AUXP, 2 * S], BF16)
                aux = now("aux", [AUXP, 4, S], BF16)
            w_dn = tmp("w_dn", [P, E, D])
            x_in = tmp("x_in", [P, 4, D])
            xt = tmp("xt", [P, 2, KC, P])
        pt = sb("pt", [P, 2, HG, CH])
        sums = sb("sums", [P, 2, NG, HG * S // P])
        inv = sb("inv", [HG, NG, S])
        ot = sb("ot", [P, NG, S])

        def bank(n, w=CH, m=P):
            return ps[0:m, n * CH:n * CH + w]

        idb = cbf[:, 0:P]
        mask_q = cbf[:, P:2 * P]
        mask_k = cbf[:, 2 * P:3 * P]

        qkd = nc.dram_tensor("qk_parts", [2, 3, NG, HD, HG, S], BF16, kind="Internal").ap()
        auxd = nc.dram_tensor("aux_rows", [2, NG, HG, N_AUX, S], BF16, kind="Internal").ap()
        xsd = nc.dram_tensor("sorted_tokens", [SLOTS, D], F32, kind="Internal").ap()
        ysd = nc.dram_tensor("sorted_outputs", [SLOTS, D], F32, kind="Internal").ap()

        s_x = [sem(f"x_loaded{i}") for i in range(4)]
        s_w = sem("w_loaded")
        s_c = sem("consts_loaded")
        s_wo = sem("wo_loaded")
        s_ws = sem("small_weights_loaded")
        s_wgu = sem("expert_gate_up_loaded")
        s_wdn = sem("expert_down_loaded")
        s_zero = sem("zeroed")
        s_clear = sem("slots_cleared")
        s_pool = sem("pool_step")
        s_ln = sem("ln_step")
        s_std = sem("std_ready")
        s_qkb = sem("qk_bias_ready")
        s_small = sem("small_weights_high")
        s_smalll = sem("small_weights_low")
        s_xn = sem("xn_ready")
        s_job = sem("job_ready")
        s_hi = sem("hi_ready")
        s_free = sem("bank_freed")
        s_res = sem("parts_ready")
        s_mid = sem("mid_ready")
        s_parts = [sem(f"parts_stored{i}") for i in range(RING)]
        s_bias = sem("bias_permuted")
        s_id = sem("ident_loaded")
        s_aux = sem("aux_ready")
        s_auxst = sem("aux_stored")
        s_prob = sem("router_exp_ready")
        s_r = sem("router_step")
        s_picked = sem("picked_ready")
        s_rank = sem("ranks_ready")
        s_slot = sem("slots_ready")
        s_scat = sem("tokens_sorted")
        s_g1 = sem("shared_hidden_ready")
        s_th = sem("shared_tanh_ready")
        s_ta = sem("shared_step")
        s_h = sem("shared_h_ready")
        s_sh = sem("shared_out_ready")
        s_sha = sem("shared_added")
        s_xin = [sem(f"tile_loaded{i}") for i in range(4)]
        s_tx = sem("tile_transposed")
        s_xt = sem("tile_evacuated")
        s_gu = sem("tile_gate_up_ready")
        s_tt = sem("tile_tanh_ready")
        s_tstep = sem("tile_step")
        s_hh = sem("tile_h_ready")
        s_tht = sem("tile_h_transposed")
        s_ht = sem("tile_h_evacuated")
        s_dn = sem("tile_out_ready")
        s_yo = sem("tile_out_evacuated")
        s_ys = [sem(f"tile_out_stored{i}") for i in range(4)]
        s_ga = [sem(f"rows_gathered{i}") for i in range(4)]
        s_gw = sem("rows_weighed")
        s_gad = sem("rows_added")
        s_ld = [[[sem(f"{side}_half{half}_loaded{p}") for p in range(2)] for half in range(2)] for side in "qk"]
        s_first = [[[sem(f"first_{side}_half{half}_loaded{p}") for p in range(2)] for half in range(2)] for side in "qk"]
        s_vg = sem("vg_ready")
        s_mxr = sem("max_scores_ready")
        s_mxf = sem("max_slot_freed")
        s_nstep = sem("neg_step")
        s_n = sem("neg_ready")
        s_nl = [sem(f"neg_loaded{p}") for p in range(2)]
        s_st = sem("scores_ready")
        s_exp = sem("exp_done")
        s_pv = sem("pv_done")
        s_ev = sem("out_evacuated")
        s_sums = [sem(f"sums_spread{i}") for i in range(3)]
        s_rec = sem("sums_inverted")
        s_invd = [sem(f"inverted_sums_in_rows{g}") for g in range(NG)]
        s_fin = sem("final_step_ready")
        s_inv = sem("final_bank_freed")
        s_y = sem("y_stored")

        block = ctx.enter_context(nc.Block())

        JOBS = ([("w", kc, c) for kc in range(KC) for c in range(3)] + [("o", oc, 0) for oc in range(2)]
                + [("b", 0, 0)] + [("x", n, 0) for n in range(TT // 2)]
                + [("g", n, 0) for n in range(T // CH)] + [("r", 0, 0)]
                + [("qk", fc, tc) for tc in range(2) for fc in range(4)] + [("k", 0, 0)]
                + [("qk", fc, tc) for tc in range(2, 4) for fc in range(4)] + [("v", n, 0) for n in range(TT // 2)])
        at = {kind: next(n for n, j in enumerate(JOBS) if j[0] == kind) for kind in ("x", "g")}
        X0, G0 = at["x"], at["g"]
        QKJ = [n for n, j in enumerate(JOBS) if j[0] == "qk"]
        NJ, NQK = len(JOBS), len(QKJ)
        HI_OF = [sum(j[0] in ("w", "x", "qk") for j in JOBS[:n + 1]) for n in range(NJ)]
        OUT_BANK = 3
        EXP_CREDIT, PV_CREDIT, MX_CREDIT = 3, 2, 2
        DMA = 16
        N_CONST = 10
        LOADS = 4
        SC = HD ** -0.5

        def load(queue, side, g, par, half, loaded):
            dst, order, done = (qs, ks)[side], (Q_PARTS, K_PARTS)[side], loaded[side][half][par]
            cols = slice(half * CH, (half + 1) * CH)
            for t0, n in ((0, 3), (3, 2), (5, 1)):
                p0 = order[t0]
                if side == 0:
                    src = qkd[0, p0:p0 + 1, bass.ds(g, 1), :, :, cols].rearrange("n g d j s -> (g n) d j s")
                    src = src.broadcast_to([n, HD, HG, CH])
                else:
                    src = qkd[1, 0:n, bass.ds(g, 1), :, :, cols].rearrange("n g d j s -> (g n) d j s")
                queue.dma_start(dst[HD * t0:HD * (t0 + n), par, :, cols], src).then_inc(done, DMA)
            rows = (N_ALIBI, N_AUX)[side]
            queue.dma_start(dst[AUX0:AUX0 + rows, par, :, cols],
                         auxd[side, bass.ds(g, 1), :, 0:rows, cols].rearrange("g j r s -> r (g j) s")
                         ).then_inc(done, DMA)

        @block.sync
        def _(sp):
            sp.dma_start(w_nat[:, :, :], qkv_w.rearrange("(c p) k -> p c k", p=P)).then_inc(s_w, DMA)
            xv = x.rearrange("b (t p) d -> p (b t) d", p=P)
            for n in range(4):
                sp.dma_start(x_sb[:, 4 * n:4 * n + 4, :], xv[:, 4 * n:4 * n + 4, :]).then_inc(s_x[n], DMA)
            sp.wait_ge(s_zero, 3)
            sp.wait_ge(s_c, DMA * N_CONST)
            sp.wait_ge(s_wo, 3 * DMA)
            sp.wait_ge(s_ws, 4 * DMA)
            xz = xsd.rearrange("(p k) d -> p (k d)", p=P)
            for n in range(NT // 4):
                sp.dma_start(xz[:, n * 4 * D:(n + 1) * 4 * D], y_out[:, :, :].rearrange("p k d -> p (k d)")
                             ).then_inc(s_clear, DMA)
            for n in range(4):
                side, half = n // 2, n % 2
                sp.wait_ge(s_aux, n + 1)
                for b in range(B):
                    sp.dma_start(auxd[side, b * 4 + 2 * half:b * 4 + 2 * half + 2].rearrange("g j r s -> (g j r) s"),
                                 aux[:, n, :]).then_inc(s_auxst, DMA)
            sp.wait_ge(s_job, X0)
            sp.wait_ge(s_auxst, 4 * B * DMA)
            sp.dma_start(w_dn[:, :, :], e_dn.rearrange("e f d -> f e d")).then_inc(s_wdn, DMA)
            for i in range(NQK):
                _, fc, tc = JOBS[QKJ[i]]
                side, g0 = fc // 2, tc // 2 * 4 + fc % 2 * 2
                cols = slice(tc % 2 * CH, (tc % 2 + 1) * CH)
                sp.wait_ge(s_res, i + 1)
                sp.dma_start(qkd[side, :, g0:g0 + 2, :, :, cols].rearrange("n g d j s -> (g d j) n s"),
                             parts[:, i % RING, :, :]).then_inc(s_parts[i % RING], DMA)
            for stored in s_parts:
                sp.wait_ge(stored, DMA * NQK // RING)
            sp.dma_start(w_gu[:, :, :, :], e_gu.rearrange("e (c p) f -> p e c f", p=P)).then_inc(s_wgu, DMA)
            sp.wait_ge(s_scat, K_TOP * TT * DMA)

            def load_tile(k, u):
                sp.dma_start(x_in[:, u, :], xsd[bass.ds(k * P, P), :]).then_inc(s_xin[u], DMA)

            def store_tile(k, u):
                sp.wait_ge(s_yo, k + 1)
                sp.dma_start(ysd[bass.ds(k * P, P), :], y_out[:, u, :]).then_inc(s_ys[u], DMA)

            for k in range(4):
                load_tile(k, k)
            def store_neg(g, par):
                sp.wait_ge(s_n, g + 1)
                for r in range(3):
                    sp.dma_start(qs[N0 + r:N0 + r + 1, par, :, :].rearrange("o j (t c) -> o (j t) c", c=P),
                                 nr[:, par, r, :]).then_inc(s_nl[par], DMA)

            def next_tile(k, u):
                sp.wait_ge(s_tx, k - 3)
                load_tile(k, u)

            for k in range(4, 7):
                next_tile(k, k % 4)
            with sp.Fori(0, NT // 4 - 2) as i:
                for u in range(4):
                    next_tile(i * 4 + u + 7, (u + 3) % 4)
                    store_tile(i * 4 + u, u)
            next_tile(NT - 1, 3)
            for k in range(NT - 8, NT):
                store_tile(k, k % 4)
            store_neg(0, 0)

            def group(g, par, ahead):
                if ahead >= 2:
                    sp.wait_ge(s_st, g * (HG * NS) + HG * 4)
                    load(sp, 0, g + 2, par, 0, s_ld)
                    sp.wait_ge(s_st, g * (HG * NS) + HG * 8)
                    load(sp, 1, g + 2, par, 0, s_ld)
                if ahead >= 1:
                    store_neg(g + 1, 1 - par)
                if ahead >= 2:
                    sp.wait_ge(s_st, g * (HG * NS) + HG * NS)
                    load(sp, 0, g + 2, par, 1, s_ld)
                    load(sp, 1, g + 2, par, 1, s_ld)

            with sp.Fori(0, NG // 2 - 1) as i:
                group(i * 2, 0, 2)
                group(i * 2 + 1, 1, 2)
            group(NG - 2, 0, 1)
            for g in range(NG):
                sp.wait_ge(s_rec, max(0, g - (NG - 3)) + 1)
                sp.dma_start(inv[:, g, :].rearrange("j (c s) -> j c s", s=HG * S // P), sums[:, 1, g, :]
                             ).then_inc(s_invd[g], DMA)
            yv = y.rearrange("b (t p) d -> p (b t) d", p=P)
            for t in range(TT):
                sp.wait_ge(s_inv, FINAL.index(("project", t)) + 1)
                sp.dma_start(yv[:, t, :], x_sb[:, t, :]).then_inc(s_y, DMA)
            sp.wait_ge(s_y, DMA * TT)

        @block.gpsimd
        def _(pool):
            g_ = nc.gpsimd
            step = [0]

            def link(ins):
                ins.then_inc(s_pool, 1)
                step[0] += 1
                pool.wait_ge(s_pool, step[0])

            g_.memset(y_out[:, :, :], 0.0).then_inc(s_zero, 1)
            g_.memset(wo_nat[:, :, :, :, :], 0.0).then_inc(s_zero, 1)
            g_.memset(eps_t[:, :], LN_EPS).then_inc(s_zero, 1)
            g_.memset(mv_pad[:, 0:1], 0.0).then_inc(s_pv, PV_CREDIT)
            g_.memset(mv_pad[:, 1:2], 0.0).then_inc(s_ev, 1)
            for n in range(8):
                g_.memset(mv_pad[:, 3 + n:4 + n], 0.0).then_inc(s_ld[n // 4][n // 2 % 2][n % 2], LOADS * DMA)
            link(g_.memset(vg[:, :, :, :, :], 0.0))
            link(g_.memset(vg[:, :, :, :, HD:HD + 1], 1.0))
            pool.wait_ge(s_c, DMA * N_CONST)
            g_.tensor_copy(qkb_row[:, :].rearrange("p (g d j) -> p g j d", j=HG, d=HD),
                           qkb_in[:, :].rearrange("p (g j d) -> p g j d", j=HG, d=HD)).then_inc(s_bias, 1)
            link(g_.tensor_copy(sl[:, 0, :], slope_in[:, :]))
            link(g_.tensor_tensor(slr[:, 1, :], slope_in[:, :], sl[:, 0, :], ALU.subtract))
            link(g_.tensor_copy(sl[:, 1, :], slr[:, 1, :]))
            link(g_.tensor_tensor(slr[:, 2, :], slr[:, 1, :], sl[:, 1, :], ALU.subtract))
            link(g_.tensor_copy(sl[:, 2, :], slr[:, 2, :]))
            for side in range(2):
                c = coef_t[:, 4 * side:4 * side + 4]
                link(g_.tensor_scalar(cq[:, side, :], sl[:, 0, :], c[:, 0:1], c[:, 3:4], ALU.mult, ALU.add))
                for k in (1, 2):
                    link(g_.tensor_scalar(slr[:, 0, :], sl[:, k, :], c[:, k:k + 1], None, ALU.mult))
                    link(g_.tensor_tensor(cq[:, side, :], cq[:, side, :], slr[:, 0, :], ALU.add))
            pool.wait_ge(s_slot, 1)
            pool.wait_ge(s_clear, NT // 4 * DMA)
            for t in range(TT):
                for k in range(K_TOP):
                    g_.indirect_dma_start(out=xsd, out_offset=bass.IndirectOffsetOnAxis(ap=slot_i[:, k, t:t + 1], axis=0),
                                          in_=xn[:, t, :], in_offset=None).then_inc(s_scat, DMA)

            def copy_v(g, par):
                g_.tensor_copy(vg[:, par, :, :, 0:HD],
                               v_sb[:, bass.ds(g, 1), :, :].rearrange("p g t (j d) -> p (g t) j d", d=HD)
                               ).then_inc(s_vg, 1)

            pool.wait_ge(s_free, NJ)
            copy_v(0, 0)
            copy_v(1, 1)
            pool.wait_ge(s_sh, TT // 2)
            for stored in s_parts:
                pool.wait_ge(stored, DMA * NQK // RING)
            for g in range(2):
                for half in range(2):
                    load(pool, 0, g, g, half, s_first)
                    load(pool, 1, g, g, half, s_first)
            for u in range(4):
                pool.wait_ge(s_ys[u], NT // 4 * DMA)
            pool.wait_ge(s_sha, TT // 2)

            def copy_next(i, par):
                pool.wait_ge(s_pv, PV_CREDIT + i * (2 * NS) + NS * (par + 1))
                copy_v(i * 2 + par + 2, par)

            def gather(n):
                t, k = n // K_TOP, n % K_TOP
                g_.indirect_dma_start(out=yg[:, n % 4, :], out_offset=None, in_=ysd,
                                      in_offset=bass.IndirectOffsetOnAxis(ap=slot_i[:, k, t:t + 1], axis=0)
                                      ).then_inc(s_ga[n % 4], DMA)

            for n in range(3):
                gather(n)
            for n in range(K_TOP * TT):
                if n == K_TOP * TT // 2:
                    copy_next(0, 0)
                if n + 3 < K_TOP * TT:
                    if n >= 1:
                        pool.wait_ge(s_gad, n)
                    gather(n + 3)
                t, k = n // K_TOP, n % K_TOP
                pool.wait_ge(s_ga[n % 4], DMA * (n // 4 + 1))
                g_.tensor_scalar(yg[:, n % 4, :], yg[:, n % 4, :], gates[:, k, t:t + 1], None, ALU.mult
                                 ).then_inc(s_gw, 1)
                pool.wait_ge(s_gw, n + 1)
                if n >= 1:
                    pool.wait_ge(s_gad, n)
                g_.tensor_tensor(x_sb[:, t, :], x_sb[:, t, :], yg[:, n % 4, :], ALU.add).then_inc(s_gad, 1)
            def spread_sums(g, spread):
                pool.wait_ge(s_ev, g * 2 + 3)
                pool.dma_start(sums[:, 0, bass.ds(g, 1), :].rearrange("p g s -> p (g s)"),
                               ot[HD::32, bass.ds(g, 1), :].rearrange("j g (c s) -> j (g c) s", s=HG * S // P)
                               ).then_inc(spread, DMA)

            copy_next(0, 1)
            for g in range(2):
                spread_sums(g, s_sums[0])
            with pool.Fori(1, NG // 2 - 1) as i:
                for par in range(2):
                    copy_next(i, par)
                    spread_sums(i * 2 + par, s_sums[0])
            for g in range(NG - 2, NG):
                spread_sums(g, s_sums[g - (NG - 3)])

        @block.scalar
        def _(act):
            sc = nc.scalar
            act.dma_start(ident[:, :], c_ident).then_inc(s_id, DMA)
            act.dma_start(perm[:, :], c_perm).then_inc(s_id, DMA)
            for dst, src in ((cbf, c_bf), (pos_t, c_pos), (coef_t, c_coef), (sel, c_sel)):
                act.dma_start(dst[:, :], src).then_inc(s_c, DMA)
            for half in range(2):
                heads = slopes[half * H // 2:(half + 1) * H // 2].rearrange("(h o) -> h o", o=1)
                act.dma_start(slope_in[:, half:half + 1], heads.unsqueeze(1).broadcast_to([H // 2, N_AUX, 1])
                              ).then_inc(s_c, DMA)
            act.dma_start(qkb_in[:, :], qkv_b[0:2 * D].rearrange("(c p) -> c p", p=P)).then_inc(s_c, DMA)
            act.dma_start(vb[:, :], qkv_b[2 * D:3 * D].partition_broadcast(P)).then_inc(s_c, DMA)
            act.dma_start(row[:, :], c_row.partition_broadcast(P)).then_inc(s_c, DMA)
            act.dma_start(eb[:, :], ebias.partition_broadcast(P)).then_inc(s_c, DMA)
            act.wait_ge(s_zero, 2)
            for oc in range(KC):
                act.dma_start(wo_nat[:, oc, :, :, 0:HD].rearrange("p g j d -> p (g j) d"),
                              out_w[oc * P:(oc + 1) * P, :].rearrange("p (h d) -> p h d", d=HD)).then_inc(s_wo, DMA)
            act.dma_start(wo_nat[:, :, 0, 0, HD:HD + 1].rearrange("p c o -> p (c o)"),
                          out_b.rearrange("(c p) -> p c", p=P), allow_slow_non_contiguous=True).then_inc(s_wo, DMA)
            act.dma_start(gw[:, :, :], gate_w.rearrange("(c p) e -> p c e", p=P)).then_inc(s_ws, DMA)
            act.dma_start(ws[:, :, 0, :], sg_w.rearrange("(c p) f -> p c f", p=P)).then_inc(s_ws, DMA)
            act.dma_start(ws[:, :, 1, :], su_w.rearrange("(c p) f -> p c f", p=P)).then_inc(s_ws, DMA)
            act.dma_start(wsd[:, :], sd_w).then_inc(s_ws, DMA)

            def high(n):
                kind, a, b = JOBS[n]
                src = bank(n % 8)
                if kind in ("w", "x", "qk", "r"):
                    act.wait_ge(s_job, n + 1)
                if kind == "w":
                    sc.activation(wh[:, a, b * D:(b + 1) * D], src[:, 0:D], ACT.Copy,
                                  scale=SC if b == 0 else 1.0).then_inc(s_hi, 1)
                elif kind == "x":
                    dst = xh[:, :, 2 * a * P:(2 * a + 2) * P].rearrange("p c (t n) -> p t c n", n=P)
                    sc.activation(dst, src.rearrange("p (t c n) -> p t c n", t=2, c=KC), ACT.Copy).then_inc(s_hi, 1)
                elif kind == "r":
                    sc.activation(prob[:, :, :], src[:, 0:TT * E].rearrange("p (t e) -> p t e", e=E), ACT.Exp,
                                  scale=-1.0).then_inc(s_prob, 1)
                elif kind == "qk":
                    i = QKJ.index(n)
                    if i == 0:
                        act.wait_ge(s_qkb, 2)
                    if i >= RING:
                        act.wait_ge(s_parts[i % RING], DMA * (i // RING))
                    sc.activation(parts[:, i % RING, 0, :], src, ACT.Identity, bias=qkb[:, a:a + 1]).then_inc(s_hi, 1)
                    if i:
                        middle(i - 1)

            def middle(i):
                act.wait_ge(s_free, QKJ[i] + 1)
                sc.activation(parts[:, i % RING, 1, :], part_r[:, i % RING, :], ACT.Copy).then_inc(s_mid, 1)

            for n in range(X0):
                high(n)
            act.wait_ge(s_ln, 2 * TT)
            act.wait_ge(s_zero, 3)
            sc.activation(std[:, :], mv[:, :, 1], ACT.Sqrt, bias=eps_t[:, :]).then_inc(s_std, 1)
            for n in range(X0, G0):
                high(n)
            act.wait_ge(s_ws, 4 * DMA)
            sc.activation(gwh[:, :, :], gw[:, :, :], ACT.Copy).then_inc(s_small, 1)
            sc.activation(wsh[:, :, :, :], ws[:, :, :, :], ACT.Copy).then_inc(s_small, 1)
            for n in range(G0, NJ):
                high(n)
            middle(NQK - 1)
            for c in range(4):
                act.wait_ge(s_g1, c + 1)
                if c >= 2:
                    act.wait_ge(s_h, c - 1)
                sc.activation(th[:, c % 2, :], bank(2 * c), ACT.Tanh, scale=0.5).then_inc(s_th, 1)

            def evacuate_x(k, v):
                act.wait_ge(s_tx, k + 1)
                sc.activation(xt[:, v, :, :], bank(v, KC * P).rearrange("p (c n) -> p c n", c=KC), ACT.Copy
                              ).then_inc(s_xt, 1)

            def tile_tanh(k, v):
                act.wait_ge(s_gu, k + 1)
                sc.activation(te_h[:, v, :], bank(2 + v, F), ACT.Tanh, scale=0.5).then_inc(s_tt, 1)

            def tile_step(k, u, left):
                v = u % 2
                act.wait_ge(s_tht, k + 1)
                sc.activation(ht[:, v, :], bank(4 + v, P), ACT.Copy).then_inc(s_ht, 1)
                if left > 2:
                    tile_tanh(k + 2, v)
                if left > 3:
                    evacuate_x(k + 3, 1 - v)

            for k in range(2):
                evacuate_x(k, k)
            for k in range(2):
                tile_tanh(k, k)
            evacuate_x(2, 0)
            with act.Fori(0, NT // 4 - 1) as i:
                for u in range(4):
                    tile_step(i * 4 + u, u, 4 + 3)
            for u in range(4):
                tile_step(NT - 4 + u, u, 4 - u)
            sc.activation(std[:, 0:1], std[:, 1:2], ACT.Exp).then_inc(s_exp, EXP_CREDIT)

            def exps(g, s, par):
                qc, kb = STEPS[s]
                lo = max(0, kb * P - qc * CH)
                for j in range(HG):
                    n = HG * s + j
                    act.wait_ge(s_st, g * (HG * NS) + n + 1)
                    if j == 0:
                        act.wait_ge(s_pv, g * NS + s + 1)
                    sc.activation(pt[:, s % 2, j, lo:CH], bank(n % 3)[:, lo:CH], ACT.Exp).then_inc(s_exp, 1)

            def evacuate(g, qc):
                act.wait_ge(s_pv, PV_CREDIT + g * NS + (4 if qc == 0 else NS))
                sc.activation(ot[:, bass.ds(g, 1), qc * CH:(qc + 1) * CH].rearrange("p g s -> p (g s)"),
                              bank(OUT_BANK), ACT.Copy).then_inc(s_ev, 1)

            def pair(g):
                for s in range(2 * NS):
                    par, st = s // NS, s % NS
                    exps(g + par, st, par)
                    if st == 4:
                        evacuate(g + par, 0)
                    if s == NS:
                        evacuate(g, 1)
                evacuate(g + 1, 1)

            with act.Fori(0, NG // 2 - 1) as i:
                pair(i * 2)
            pair(NG - 2)

        @block.vector
        def _(dve):
            v = nc.vector
            v.memset(mx[:, :, :], 0.0).then_inc(s_mxf, MX_CREDIT)
            for t in range(TT):
                if t % 4 == 0:
                    dve.wait_ge(s_x[t // 4], DMA)
                v.bn_stats(stats[:, t, :], x_sb[:, t, :]).then_inc(s_ln, 1)
            for t in range(TT):
                dve.wait_ge(s_ln, t + 1)
                v.bn_aggr(mv[:, t, :], stats[:, t, :]).then_inc(s_ln, 1)

            def last_part(i):
                dve.wait_ge(s_mid, i + 1)
                v.tensor_tensor(parts[:, i % RING, 2, :], part_r[:, i % RING, :], parts[:, i % RING, 1, :],
                                ALU.subtract).then_inc(s_res, 1)

            def low(n):
                kind, a, b = JOBS[n]
                dve.wait_ge(s_job, n + 1)
                src = bank(n % 8)
                if kind == "w":
                    dve.wait_ge(s_hi, HI_OF[n])
                    v.scalar_tensor_tensor(wl[:, a, b * D:(b + 1) * D], src[:, 0:D], SC if b == 0 else 1.0,
                                           wh[:, a, b * D:(b + 1) * D], ALU.mult, ALU.subtract).then_inc(s_free, 1)
                elif kind == "o":
                    v.tensor_copy(wo_t[:, :, a * P:(a + 1) * P],
                                  src.rearrange("p (g n) -> p g n", n=P)).then_inc(s_free, 1)
                elif kind == "b":
                    v.tensor_scalar(qkb[:, 0:2], src[:, 0:2], SC, None, ALU.mult).then_inc(s_qkb, 1)
                    v.tensor_copy(qkb[:, 2:4], src[:, 2:4]).then_inc(s_qkb, 1)
                    dve.wait_ge(s_qkb, 2)
                    v.memset(mv_pad[:, 2:3], 0.0).then_inc(s_free, 1)
                elif kind == "x":
                    dve.wait_ge(s_hi, HI_OF[n])
                    cols = slice(2 * a * P, (2 * a + 2) * P)
                    v.tensor_tensor(xl[:, :, cols].rearrange("p c (t n) -> p t c n", n=P),
                                    src.rearrange("p (t c n) -> p t c n", t=2, c=KC),
                                    xh[:, :, cols].rearrange("p c (t n) -> p t c n", n=P),
                                    ALU.subtract).then_inc(s_free, 1)
                elif kind == "g":
                    v.tensor_copy(logits_t[:, a * CH:(a + 1) * CH], src[0:E, :]).then_inc(s_free, 1)
                elif kind == "r":
                    route()
                elif kind == "k":
                    place()
                elif kind == "qk":
                    i = QKJ.index(n)
                    dve.wait_ge(s_hi, HI_OF[n])
                    v.scalar_tensor_tensor(part_r[:, i % RING, :], src, qkb[:, a:a + 1], parts[:, i % RING, 0, :],
                                           ALU.add, ALU.subtract).then_inc(s_free, 1)
                    if i:
                        last_part(i - 1)
                else:
                    t = 2 * a
                    b_, kb = t // QT, t % QT
                    dst = v_sb[:, 4 * b_:4 * b_ + 4, kb:kb + 2, :].rearrange("p g t n -> p t g n")
                    v.tensor_tensor(dst, src.rearrange("p (t g n) -> p t g n", t=2, g=4),
                                    vb[:, :].rearrange("p (o g n) -> p o g n", o=1, g=4).to_broadcast([P, 2, 4, HG * HD]),
                                    ALU.add).then_inc(s_free, 1)

            steps = [0]

            def then(ins):
                ins.then_inc(s_r, 1)
                steps[0] += 1
                dve.wait_ge(s_r, steps[0])

            def over_e(ap):
                return ap.unsqueeze(2).broadcast_to([P, TT, E])

            def over_t(ap):
                return ap.unsqueeze(1).broadcast_to([P, TT, E])

            rank_row = row[:, 0:E]
            before = row[:, E:E + E * E].rearrange("p (a b) -> p a b", b=E)
            fills = row[:, E + E * E:E + 2 * E * E].rearrange("p (a b) -> p a b", b=E)
            tile_no = row[:, E + 2 * E * E:].rearrange("p (k e) -> p k e", e=E)

            def route():
                dve.wait_ge(s_prob, 1)
                then(v.tensor_scalar(rt[:, :, :], prob[:, :, :], 1.0, None, ALU.add))
                then(v.reciprocal(prob[:, :, :], rt[:, :, :]))
                then(v.tensor_tensor(biased[:, :, :], prob[:, :, :], over_t(eb[:, :]), ALU.add))
                for k in range(K_TOP):
                    p_ = pick[:, k, :, :]
                    then(v.reduce_max(top[:, 0, :], biased[:, :, :], axis=AX.X))
                    then(v.tensor_tensor(rt[:, :, :], biased[:, :, :], over_e(top[:, 0, :]), ALU.is_equal))
                    then(v.tensor_tensor(rt[:, :, :], rt[:, :, :], over_t(rank_row), ALU.mult))
                    then(v.reduce_max(top[:, 1, :], rt[:, :, :], axis=AX.X))
                    then(v.tensor_tensor(p_, rt[:, :, :], over_e(top[:, 1, :]), ALU.is_equal))
                    if k == 0:
                        then(v.scalar_tensor_tensor(biased[:, :, :], p_, NEG, biased[:, :, :], ALU.mult, ALU.add))
                v.tensor_tensor(picked[:, :, :], pick[:, 0, :, :], pick[:, 1, :, :], ALU.add).then_inc(s_picked, 1)
                for k in range(K_TOP):
                    then(v.tensor_tensor(rt[:, :, :], pick[:, k, :, :], prob[:, :, :], ALU.mult))
                    then(v.reduce_sum(top[:, 2 + k, :], rt[:, :, :], axis=AX.X))
                then(v.scalar_tensor_tensor(top[:, 4, :], top[:, 2, :], 1e-20, top[:, 3, :], ALU.add, ALU.add))
                then(v.reciprocal(top[:, 5, :], top[:, 4, :]))
                for k in range(K_TOP):
                    then(v.tensor_tensor(gates[:, k, :], top[:, 2 + k, :], top[:, 5, :], ALU.mult))
                v.memset(mv_pad[:, 11:12], 0.0).then_inc(s_free, 1)

            def place():
                ranks = bank(JOBS.index(("k", 0, 0)) % 8)
                counts = ranks[:, TT * E:TT * E + E]
                sq = [P, E, E]
                then(v.tensor_tensor(rt[:, :, :], counts.unsqueeze(2).broadcast_to(sq), fills, ALU.is_gt))
                then(v.reduce_sum(cnt[:, 0, :], rt[:, :, :], axis=AX.X))
                then(v.tensor_tensor(rt[:, :, :], cnt[:, 0, :].unsqueeze(1).broadcast_to(sq), before, ALU.mult))
                then(v.reduce_sum(cnt[:, 1, :], rt[:, :, :], axis=AX.X))
                then(v.tensor_tensor(cnt[:, 2, :], cnt[:, 0, :], cnt[:, 1, :], ALU.add))
                then(v.tensor_scalar(cnt[:, 3, :], cnt[:, 1, :], float(P), None, ALU.mult))
                then(v.tensor_tensor(rt[:, :, :], ranks[:, 0:TT * E].rearrange("p (t e) -> p t e", e=E),
                                     over_t(cnt[:, 3, :]), ALU.add))
                for k in range(K_TOP):
                    then(v.tensor_tensor(biased[:, :, :], pick[:, k, :, :], rt[:, :, :], ALU.mult))
                    then(v.reduce_sum(slot_f[:, k, :], biased[:, :, :], axis=AX.X))
                v.tensor_copy(slot_i[:, :, :], slot_f[:, :, :]).then_inc(s_slot, 1)
                et = etab[:, :].rearrange("p (k e) -> p k e", e=E)
                then(v.tensor_tensor(et, cnt[:, 2, :].unsqueeze(1).broadcast_to([P, NT, E]), tile_no, ALU.is_le))
                then(v.reduce_sum(eid_f[:, :], et, axis=AX.X))
                v.tensor_scalar(eid[:, :], eid_f[:, :], float(E - 1), None, ALU.min).then_inc(s_free, 1)

            for n in range(X0):
                low(n)
            dve.wait_ge(s_std, 1)
            v.reciprocal(rstd[:, :], std[:, :]).then_inc(s_ln, 1)
            dve.wait_ge(s_ln, 2 * TT + 1)
            for t in range(TT):
                v.tensor_scalar(xn[:, t, :], x_sb[:, t, :], mv[:, t, 0:1], rstd[:, t:t + 1],
                                ALU.subtract, ALU.mult).then_inc(s_xn, 1)
            for n in range(X0, G0):
                low(n)
            dve.wait_ge(s_small, 2)
            v.tensor_tensor(gwl[:, :, :], gw[:, :, :], gwh[:, :, :], ALU.subtract).then_inc(s_smalll, 1)
            v.tensor_tensor(wsl[:, :, :, :], ws[:, :, :, :], wsh[:, :, :, :], ALU.subtract).then_inc(s_smalll, 1)
            dve.wait_ge(s_pool, 2 + 5 + 10)
            for n in range(4):
                side, half = n // 2, n % 2
                v.tensor_scalar(aux[:, n, :], pos_t[:, side * S:(side + 1) * S], cq[:, side, half:half + 1], None,
                                ALU.mult).then_inc(s_aux, 1)
            for n in range(G0, NJ):
                low(n)
                if n == QKJ[-1]:
                    last_part(NQK - 1)
            for c in range(4):
                dve.wait_ge(s_th, c + 1)
                v.scalar_tensor_tensor(th[:, c % 2, :], th[:, c % 2, :], 1.0, bank(2 * c), ALU.add, ALU.mult
                                       ).then_inc(s_ta, 1)
                dve.wait_ge(s_ta, c + 1)
                if c >= 2:
                    dve.wait_ge(s_sh, 2 * (c - 1))
                v.scalar_tensor_tensor(hsh[:, c % 2, :], th[:, c % 2, :], 0.5, bank(2 * c + 1), ALU.mult, ALU.mult
                                       ).then_inc(s_h, 1)
            for n in range(TT // 2):
                dve.wait_ge(s_sh, n + 1)
                xs = x_sb[:, 2 * n:2 * n + 2, :].rearrange("p t d -> p (t d)")
                v.tensor_tensor(xs, xs, bank(n), ALU.add).then_inc(s_sha, 1)

            def tile_hidden(k, w):
                dve.wait_ge(s_tt, k + 1)
                v.scalar_tensor_tensor(te_h[:, w, :], te_h[:, w, :], 1.0, bank(2 + w, F), ALU.add, ALU.mult
                                       ).then_inc(s_tstep, 1)
                dve.wait_ge(s_tstep, k + 1)
                v.scalar_tensor_tensor(hh[:, w, :], te_h[:, w, :], 0.5, ps[:, (2 + w) * CH + F:(2 + w) * CH + 2 * F],
                                       ALU.mult, ALU.mult).then_inc(s_hh, 1)

            def tile_step(k, u, left, stored):
                dve.wait_ge(s_dn, k + 1)
                if stored is not None:
                    dve.wait_ge(s_ys[u], stored)
                v.tensor_copy(y_out[:, u, :], bank(6 + u % 2, D)).then_inc(s_yo, 1)
                if left > 2:
                    tile_hidden(k + 2, u % 2)

            for k in range(2):
                tile_hidden(k, k)
            for u in range(4):
                tile_step(u, u, 4, None)
            with dve.Fori(1, NT // 4 - 1) as i:
                for u in range(4):
                    tile_step(i * 4 + u, u, 4, i * DMA)
            for u in range(4):
                tile_step(NT - 4 + u, u, 4 - u, (NT // 4 - 1) * DMA)

            def maxima(g, par, p):
                n = g * NP + p
                qt, j0, nj = PIECES[p]
                w = (qt + 1) * P
                dve.wait_ge(s_mxr, n + 1)
                src = ps[:, (4 + 2 * (p % 2)) * CH:(4 + 2 * (p % 2)) * CH + nj * w].rearrange("p (j w) -> p j w", j=nj)
                dst = mx[:, par, :].rearrange("p (j t) -> p j t", j=HG)[:, j0:j0 + nj, qt]
                last = v.reduce_max(dst, src, axis=AX.X)
                last.then_inc(s_mxf, 1)

            def negate(g, par):
                dve.wait_ge(s_mxr, (g + 1) * NP)
                src = bank(6, P, HG * QT)
                v.tensor_scalar(nr[:, par, 0, :], src, -1.0, None, ALU.mult).then_inc(s_nstep, 1)
                dve.wait_ge(s_nstep, g * 2 + 1)
                v.scalar_tensor_tensor(nrf[:, par, :], src, -1.0, nr[:, par, 0, :], ALU.mult,
                                       ALU.subtract).then_inc(s_mxf, 1)
                dve.wait_ge(s_mxf, MX_CREDIT + (g + 1) * NP)
                v.tensor_copy(nr[:, par, 1, :], nrf[:, par, :]).then_inc(s_nstep, 1)
                dve.wait_ge(s_nstep, g * 2 + 2)
                v.tensor_tensor(nr[:, par, 2, :], nrf[:, par, :], nr[:, par, 1, :], ALU.subtract).then_inc(s_n, 1)

            def beside(g, par, ahead):
                for dg, p in [x[1:] for x in ORDER if x[0] == "max"]:
                    if dg > ahead:
                        continue
                    q = (par + dg) % 2
                    if p == NP - 1:
                        negate(g + dg, q)
                    else:
                        maxima(g + dg, q, p)

            for p in range(NP - 1):
                maxima(0, 0, p)
            negate(0, 0)
            for p in range(EARLY):
                maxima(1, 1, p)

            with dve.Fori(0, NG // 2 - 1) as i:
                for par in range(2):
                    beside(i * 2 + par, par, 2)
            beside(NG - 2, 0, 1)
            def invert(g0, g1):
                dve.wait_ge(s_sums[max(0, g0 - (NG - 3))], (g1 - g0) * DMA)
                v.reciprocal(sums[:, 1, g0:g1, :], sums[:, 0, g0:g1, :]).then_inc(s_rec, 1)

            invert(0, NG - 2)
            invert(NG - 2, NG - 1)
            dve.wait_ge(s_gad, K_TOP * TT)
            for m, (kind, n) in enumerate(FINAL):
                if m == SUMS_AT:
                    invert(NG - 1, NG)
                dve.wait_ge(s_fin, m + 1)
                if kind == "divide":
                    o = ot[:, n // 2, n % 2 * CH:(n % 2 + 1) * CH]
                    v.tensor_tensor(o, o, bank(4 + m % 4), ALU.mult).then_inc(s_inv, 1)
                else:
                    v.tensor_tensor(x_sb[:, n, :], x_sb[:, n, :], bank(4 + m % 4, D), ALU.add).then_inc(s_inv, 1)

        @block.tensor
        def _(pe):
            te = nc.tensor

            def split_product(out, sides, first=True, last=True):
                ops = [(l, r) for (ah, al, bh, bl) in sides for l, r in ((al, bh), (ah, bl), (ah, bh))]
                for k, (l, r) in enumerate(ops):
                    ins = te.matmul(out, l, r, start=k == 0, stop=k == len(ops) - 1)
                return ins

            pe.wait_ge(s_id, 2 * DMA)
            for n, (kind, a, b) in enumerate(JOBS):
                out = bank(n % 8)
                if n >= 8:
                    pe.wait_ge(s_free, n - 7)
                if kind == "w":
                    pe.wait_ge(s_w, DMA)
                    for k in range(2):
                        ins = te.matmul(out[:, k * P:(k + 1) * P], w_nat[:, 2 * b + k, a * P:(a + 1) * P],
                                        (perm, perm, ident)[b][:, :], start=True, stop=True)
                elif kind == "o":
                    pe.wait_ge(s_wo, 3 * DMA)
                    for hg in range(H // HG):
                        ins = te.transpose(out[:, hg * P:(hg + 1) * P],
                                           wo_nat[:, a, hg, :, :].rearrange("p j d -> p (j d)"), ident[:, :])
                elif kind == "b":
                    pe.wait_ge(s_bias, 1)
                    ins = te.transpose(out[:, 0:4], qkb_row[:, :], ident[0:4, 0:4])
                elif kind == "x":
                    pe.wait_ge(s_xn, 2 * a + 2)
                    for k in range(4):
                        ins = te.transpose(out[:, k * P:(k + 1) * P],
                                           xn[:, 2 * a + k // 2, k % 2 * P:(k % 2 + 1) * P], ident[:, :])
                elif kind == "g":
                    pe.wait_ge(s_free, X0 + 2 * a + 2)
                    pe.wait_ge(s_smalll, 2)
                    ts = slice(a * CH, (a + 1) * CH)
                    ops = [(l, r) for c in range(KC)
                           for l, r in ((gwl[:, c, :], xl[:, c, ts]), (gwh[:, c, :], xl[:, c, ts]),
                                        (gwl[:, c, :], xh[:, c, ts]), (gwh[:, c, :], xh[:, c, ts]))]
                    for k, (l, r) in enumerate(ops):
                        ins = te.matmul(out[0:E, :], l, r, start=k == 0, stop=k == len(ops) - 1)
                elif kind == "r":
                    pe.wait_ge(s_free, n)
                    for t in range(TT):
                        ins = te.transpose(out[:, t * E:(t + 1) * E], logits_t[:, t * P:(t + 1) * P],
                                           ident[0:E, 0:E])
                elif kind == "k":
                    pe.wait_ge(s_c, DMA * N_CONST)
                    pe.wait_ge(s_picked, 1)
                    for t in range(TT):
                        te.matmul(out[:, TT * E:TT * E + E], cbf[:, 4 * P:5 * P], picked[:, t, :],
                                  start=t == 0, stop=t == TT - 1)
                    te.matmul(out[:, 0:TT * E], cbf[:, 3 * P:4 * P], picked[:, :, :].rearrange("p t e -> p (t e)"),
                              start=True, stop=False)
                    for t in range(TT - 1):
                        ins = te.matmul(out[:, (t + 1) * E:TT * E], cbf[:, 4 * P:5 * P],
                                        picked[:, t, :].unsqueeze(1).broadcast_to([P, TT - 1 - t, E]),
                                        start=False, stop=t == TT - 2)
                elif kind == "qk":
                    f, t = slice(a * P, (a + 1) * P), slice(b * CH, (b + 1) * CH)
                    ins = split_product(out, [(wh[:, c, f], wl[:, c, f], xh[:, c, t], xl[:, c, t]) for c in range(KC)])
                else:
                    w = slice(2 * D, 3 * D)
                    for k in range(2):
                        t = slice((2 * a + k) * P, (2 * a + k + 1) * P)
                        ins = split_product(out[:, k * D:(k + 1) * D],
                                            [(xh[:, c, t], xl[:, c, t], wh[:, c, w], wl[:, c, w]) for c in range(KC)])
                ins.then_inc(s_job, 1)

            def shared_down(c):
                pe.wait_ge(s_h, c + 1)
                for t in range(4):
                    ins = te.matmul(ps[:, 2 * c * CH + t * D:2 * c * CH + (t + 1) * D],
                                    hsh[:, c % 2, t * P:(t + 1) * P], wsd[:, :], start=True, stop=True)
                    if t % 2:
                        ins.then_inc(s_sh, 1)

            pe.wait_ge(s_free, NJ)
            for c in range(4):
                t = slice(c * CH, (c + 1) * CH)
                for k in range(2):
                    ins = split_product(bank(2 * c + k), [(wsh[:, m, k, :], wsl[:, m, k, :], xh[:, m, t], xl[:, m, t])
                                                          for m in range(KC)])
                ins.then_inc(s_g1, 1)
                if c:
                    shared_down(c - 1)
            shared_down(3)

            def tile_in(k, u, need):
                pe.wait_ge(s_xin[u], need)
                for c in range(KC):
                    ins = te.transpose(ps[:, (u % 2) * CH + c * P:(u % 2) * CH + (c + 1) * P],
                                       x_in[:, u, c * P:(c + 1) * P], ident[:, :])
                ins.then_inc(s_tx, 1)

            def expert_of(k):
                return pe.value_load(eid[0:1, bass.ds(k, 1)], min_val=0, max_val=E - 1)

            def gate_up(k, w):
                e = expert_of(k)
                pe.wait_ge(s_xt, k + 1)
                for c in range(KC):
                    ins = te.matmul(bank(2 + w, 2 * F), xt[:, w, c, :],
                                    w_gu[:, bass.ds(e, 1), c, :].rearrange("p o f -> p (o f)"),
                                    start=c == 0, stop=c == KC - 1)
                ins.then_inc(s_gu, 1)

            def tile_step(k, u, left, need):
                w = u % 2
                pe.wait_ge(s_hh, k + 1)
                te.transpose(bank(4 + w, P), hh[:, w, :], ident[:, :]).then_inc(s_tht, 1)
                if left > 2:
                    gate_up(k + 2, w)
                if left > 3:
                    tile_in(k + 3, (u + 3) % 4, need)
                e = expert_of(k)
                pe.wait_ge(s_ht, k + 1)
                te.matmul(bank(6 + w, D), ht[:, w, :], w_dn[:, bass.ds(e, 1), :].rearrange("p o f -> p (o f)"),
                          start=True, stop=True).then_inc(s_dn, 1)

            pe.wait_ge(s_sha, TT // 2)
            for k in range(2):
                tile_in(k, k, DMA)
            pe.wait_ge(s_wgu, DMA)
            pe.wait_ge(s_wdn, DMA)
            for k in range(2):
                gate_up(k, k)
            tile_in(2, 2, DMA)
            with pe.Fori(0, NT // 4 - 1) as i:
                for u in range(4):
                    tile_step(i * 4 + u, u, 4 + 3, (i + (u + 3) // 4 + 1) * DMA)
            for u in range(4):
                tile_step(NT - 4 + u, u, 4 - u, NT // 4 * DMA)
            pe.wait_ge(s_yo, NT)

            def max_scores(g, par, p):
                pe.wait_ge(s_mxf, g * NP + p + 1)
                base = (4 + 2 * (p % 2)) * CH
                if p == NP - 1:
                    pe.wait_ge(s_mxf, MX_CREDIT + g * NP + NP - 1)
                    te.transpose(bank(6, P, HG * QT), mx[:, par, :], ident[:, :]).then_inc(s_mxr, 1)
                    return
                qt, j0, nj = PIECES[p]
                w = (qt + 1) * P
                for j in range(j0, j0 + nj):
                    at = base + (j - j0) * w
                    q = qs[0:K_MAX, par, j, qt * P:(qt + 1) * P]
                    for c in range(0, w, CH):
                        e = min(w, c + CH)
                        te.matmul(ps[:, at + c:at + e], q, ks[0:K_MAX, par, j, c:e], start=True, stop=e < w)
                    ins = te.matmul(ps[:, at + w - P:at + w], idb, mask_q, start=False, stop=True)
                ins.then_inc(s_mxr, 1)

            def exp_scores(g, s, par, heads):
                qc, kb = STEPS[s]
                lo = max(0, kb * P - qc * CH)
                diag = kb * P >= qc * CH
                for j in heads:
                    n = HG * s + j
                    pe.wait_ge(s_exp, g * (HG * NS) + n + 1)
                    out = bank(n % 3)
                    ins = te.matmul(out[:, lo:CH], ks[0:K_EXP, par, j, kb * P:(kb + 1) * P],
                                    qs[0:K_EXP, par, j, qc * CH + lo:(qc + 1) * CH], start=True, stop=not diag)
                    if diag:
                        ins = te.matmul(out[:, lo:lo + P], idb, mask_k, start=False, stop=True)
                    ins.then_inc(s_st, 1)

            def weigh(g, s, par):
                qc, kb = STEPS[s]
                lo = max(0, kb * P - qc * CH)
                pe.wait_ge(s_exp, EXP_CREDIT + g * (HG * NS) + HG * (s + 1))
                if kb == 0:
                    pe.wait_ge(s_ev, g * 2 + qc + 1)
                for j in range(HG):
                    ins = te.matmul(ps[32 * j:32 * j + 32, OUT_BANK * CH + lo:(OUT_BANK + 1) * CH], vg[:, par, kb, j, :],
                                    pt[:, s % 2, j, lo:CH], start=kb == 0, stop=kb == 4 * qc + 3,
                                    tile_position=(0, 32 * j))
                ins.then_inc(s_pv, 1)


            def final(m):
                kind, n = FINAL[m]
                if m == 0:
                    pe.wait_ge(s_mxf, MX_CREDIT + NG * NP)
                if m >= 4:
                    pe.wait_ge(s_inv, m - 3)
                if kind == "divide":
                    pe.wait_ge(s_invd[n // 2], DMA)
                    ins = te.matmul(bank(4 + m % 4), sel[:, :], inv[:, n // 2, n % 2 * CH:(n % 2 + 1) * CH],
                                    start=True, stop=True)
                else:
                    if n % QT == 0:
                        pe.wait_ge(s_inv, FINAL.index(("divide", NG * (n // QT + 1) - 1)) + 1)
                    for hg in range(H // HG):
                        ins = te.matmul(bank(4 + m % 4, D), ot[:, n // QT * 4 + hg, n % QT * P:(n % QT + 1) * P],
                                        wo_t[:, hg, :], start=hg == 0, stop=hg == 3)
                ins.then_inc(s_fin, 1)

            def pair(g, last, count):
                beside = 0
                for par in range(2):
                    pe.wait_ge(s_nl[par], count * (3 * DMA))
                    pe.wait_ge(s_vg, g + par + 1)
                    for kind, a, b in [(*x, 0)[:3] for x in ORDER]:
                        if kind == "exp":
                            exp_scores(g + par, a, par, [b])
                            if last and par:
                                while beside * HG * NS < (HG * a + b - 6) * BESIDE:
                                    final(beside)
                                    beside += 1
                        elif kind == "out" and a + par:
                            weigh(g + par - (a == 0), (a - 1) % NS, par - (a == 0))
                        elif kind == "max" and not (last and a + par > 1):
                            q = (par + a) % 2
                            if b in (0, FIRST_HALF):
                                for side in range(2):
                                    pe.wait_ge(s_ld[side][int(b > 0)][q], (count + (par + a) // 2) * (LOADS * DMA))
                            max_scores(g + par + a, q, b)
                weigh(g + 1, NS - 1, 1)
                return beside

            for g, n in ((0, NP), (1, EARLY)):
                for p in range(n):
                    if p in (0, FIRST_HALF):
                        for side in range(2):
                            pe.wait_ge(s_first[side][int(p > 0)][g], LOADS * DMA)
                    max_scores(g, g, p)
            for side in range(2):
                pe.wait_ge(s_first[side][1][1], LOADS * DMA)
            with pe.Fori(0, NG // 2 - 1) as i:
                pair(i * 2, False, i + 1)
            beside = pair(NG - 2, True, NG // 2)

            for m in range(beside, len(FINAL)):
                final(m)


NAMES = {
    "L0_attn_hidden_states": "x", "L0_attn_qkv_w": "qkv_w", "L0_attn_qkv_b": "qkv_b", "L0_attn_out_w": "out_w",
    "L0_attn_out_b": "out_b", "L0_attn_alibi_slopes": "slopes", "L0_ffn_gate_w": "gate_w",
    "L0_ffn_expert_bias": "ebias", "L0_ffn_shared_gate_w": "sg_w", "L0_ffn_shared_up_w": "su_w",
    "L0_ffn_shared_down_w": "sd_w", "L0_ffn_experts_gate_up": "e_gu", "L0_ffn_experts_down": "e_dn",
}


def kernel(**inputs):
    import concourse.bacc as bacc
    from concourse.bass_utils import run_bass_kernel_spmd

    nc = bacc.Bacc("TRN2", target_bir_lowering=False, num_devices=1)
    arrays = {short: np.ascontiguousarray(inputs[name]) for name, short in NAMES.items()}
    arrays.update(constants())
    args = [nc.dram_tensor(k, a.shape, mybir.dt.from_np(a.dtype), kind="ExternalInput").ap()
            for k, a in arrays.items()]
    out = nc.dram_tensor("y", (B, S, D), F32, kind="ExternalOutput").ap()
    build(nc, *args, out)
    return run_bass_kernel_spmd(nc, [arrays], core_ids=[0]).results[0]["y"]
```

```python
from contextlib import ExitStack

import numpy as np

import concourse.bass as bass
import concourse.mybir as mybir

F32 = mybir.dt.float32
F32R = mybir.dt.float32r
BF16 = mybir.dt.bfloat16
I32 = mybir.dt.int32
ALU = mybir.AluOpType
ACT = mybir.ActivationFunctionType
AX = mybir.AxisListType

P = 128
B, S, D, H = 2, 1024, 256, 16
HD = D // H
T = B * S
TT = T // P
KC = D // P
HG = 4
E, F, K_TOP = 16, 128, 2
NT = (K_TOP * T + E * (P - 1)) // P + 1
NT = -(-NT // (4 * HG)) * (4 * HG)
NTH = NT // HG
SLOTS = NT * P
NG = B * H // HG
QT = S // P
CH = 512
NEG = -1.0e30
LN_EPS = 1e-5

Q_PARTS = (0, 0, 0, 1, 1, 2)
K_PARTS = (0, 1, 2, 0, 1, 0)
AUX0 = 6 * HD
N_ALIBI = 12
N0 = AUX0 + N_ALIBI
K_MAX = N0
K_EXP = N0 + 3
N_AUX = K_EXP - AUX0
AUXP = H // 2 * N_AUX

STEPS = [(qc, kb) for qc in range(2) for kb in range(4 * qc + 4)]
NS = len(STEPS)


def max_pieces():
    out = [(0, 0, 4), (1, 0, 2), (1, 2, 2)]
    for qt in range(2, QT):
        out += [(qt, j, 1) for j in range(HG)]
    return out


PIECES = max_pieces()
NP = len(PIECES) + 1
RING = 6
EARLY = 3


def schedule():
    items = [("exp", s, j) for s in range(NS) for j in range(HG)]
    exp_cost = [CH - max(0, STEPS[s][1] * P - STEPS[s][0] * CH) + 230 for _, s, _ in items]
    pieces = []
    for (ahead, ps), (start, end) in WINDOWS:
        cost = [(1 + PIECES[p][0]) * P * PIECES[p][2] + 200 if p < NP - 1 else 100 for p in ps]
        pieces += [(start + (end - start) * sum(cost[:n]) / sum(cost), ahead, p) for n, p in enumerate(ps)]
    pieces.sort()
    out, now = [], 0
    for item, cost in zip(items, exp_cost):
        out.append(item)
        if item[2] == OUT_AFTER:
            out.append(("out", item[1]))
        now += cost / sum(exp_cost)
        while pieces and pieces[0][0] <= now:
            out.append(("max", *pieces.pop(0)[1:]))
    return out + [("max", *x[1:]) for x in pieces]


FIRST_HALF = 11
WINDOWS = [((1, range(EARLY, FIRST_HALF)), (0.0, 0.2)), ((1, range(FIRST_HALF, NP)), (0.22, 0.88)),
           ((2, range(EARLY)), (0.9, 1.0))]
OUT_AFTER = 3
ORDER = schedule()

FIRST_AT = [(q * NTH + NTH // 2) // QT for q in range(QT)]

FINAL = ([("divide", n) for n in range(2 * NG - 2)] + [("project", t) for t in range(QT)]
         + [("divide", n) for n in range(2 * NG - 2, 2 * NG)] + [("project", t) for t in range(QT, B * QT)])
BESIDE = 2 * NG - 2 + 3
SUMS_AT = BESIDE + 1


def constants():
    bf = mybir.dt.np(BF16)
    k = np.arange(P)
    above = np.where(k[None, :] > k[:, None], NEG, 0.0)
    pos = np.arange(S)
    a, b, one = pos // 8 * 8, pos % 8, np.ones(S)
    tq = np.stack([one, a, one, b] * 3 + [one] * 3)
    tk = np.stack([a, one, b, one] * 3 + [one] * 3)
    coef = np.zeros((N_AUX, 2, 4), np.float32)
    for r in range(N_ALIBI):
        if r % 2 == 0:
            coef[r, 0, r // 4] = 1
            coef[r, 1, 3] = 1
        else:
            coef[r, 0, 3] = 1
            coef[r, 1, r // 4] = -1
    coef[N_ALIBI:, 1, 3] = 1
    e = np.arange(E)
    row = np.concatenate([E - e, (e[None, :] < e[:, None]).ravel(), np.tile(P * e, E), np.repeat(np.arange(NT), E)])
    sel = (np.arange(P)[None, :] // 32 == np.arange(3 * HG)[:, None] % HG).astype(bf)
    perm = np.zeros((P, P), np.float32)
    perm[k, k // (P // 2) * (P // 2) + k % HD * HG + k // HD % HG] = 1
    lower = (k[:, None] < k[None, :]).astype(np.float32)
    return {
        "c_ident": np.eye(P, dtype=np.float32),
        "c_perm": perm,
        "c_bf": np.concatenate([np.eye(P), above, above.T, lower, np.ones((P, P))], 1).astype(bf),
        "c_pos": np.tile(np.concatenate([tq, tk], 1), (H // 2, 1)).astype(bf),
        "c_coef": np.tile(coef.reshape(N_AUX, 8), (H // 2, 1)),
        "c_sel": sel,
        "c_row": row.astype(np.float32),
    }


def build(nc, x, qkv_w, qkv_b, out_w, out_b, slopes, gate_w, ebias, sg_w, su_w, sd_w, e_gu, e_dn,
          c_ident, c_perm, c_bf, c_pos, c_coef, c_sel, c_row, y):
    ctx = ExitStack()
    with ctx:
        def sb(name, shape, dt=F32):
            return ctx.enter_context(nc.sbuf_tensor(name, shape, dt))

        def sem(name):
            return ctx.enter_context(nc.semaphore(name))

        x_sb = sb("x_sb", [P, TT, D])
        wo_t = sb("wo_t", [P, H // HG, D])
        ident = sb("ident", [P, P])
        cbf = sb("cbf", [P, 5 * P], BF16)
        sel = sb("sel", [3 * HG, P], BF16)
        v_sb = sb("v_sb", [P, NG, QT, HG * HD])
        yg = sb("yg", [P, 4, D])
        mx = sb("mx", [P, 2, HG * QT])
        nr = sb("nr", [HG * QT, 2, 3, P], BF16)
        nrf = sb("nrf", [HG * QT, 2, P])
        slot_i = sb("slot_i", [P, K_TOP, TT], I32)
        eid = sb("eid", [P, NT], I32)
        gates = sb("gates", [P, K_TOP, TT])
        mv_pad = sb("mv_pad", [P, 11])
        vg = sb("vg", [P, 2, QT, HG, 32])
        ps = ctx.enter_context(nc.psum_tensor("ps", [P, 8 * CH], F32))

        with nc.sbuf_tensor("xh", [P, KC, T], F32R) as xh, nc.sbuf_tensor("xl", [P, KC, T], F32R) as xl:
            pass
        qs = sb("qs", [P, 2, HG, S], BF16)
        ks = sb("ks", [P, 2, HG, S], BF16)
        with ExitStack() as early:
            def tmp(name, shape, dt=F32):
                return early.enter_context(nc.sbuf_tensor(name, shape, dt))

            xn = tmp("xn", [P, TT, D])
            with ExitStack() as first:
                parts = first.enter_context(nc.sbuf_tensor("parts", [P, RING, 3, CH], BF16))
                part_r = first.enter_context(nc.sbuf_tensor("part_r", [P, RING, CH], F32))
            w_gu = tmp("w_gu", [P, E, KC, 2 * F])
            wh = tmp("wh", [P, KC, 3 * D], F32R)
            wl = tmp("wl", [P, KC, 3 * D], F32R)
            gw = tmp("gw", [P, KC, E])
            gwh = tmp("gwh", [P, KC, E], F32R)
            gwl = tmp("gwl", [P, KC, E], F32R)
            ws = tmp("ws", [P, KC, 2, F])
            wsh = tmp("wsh", [P, KC, 2, F], F32R)
            wsl = tmp("wsl", [P, KC, 2, F], F32R)
            wsd = tmp("wsd", [P, D])
            perm = tmp("perm", [P, P])
            qkb = tmp("qkb", [P, 4])
            qkb_in = tmp("qkb_in", [4, P])
            qkb_row = tmp("qkb_row", [4, P])
            vb = tmp("vb", [P, D])
            eb = tmp("eb", [P, E])
            row = tmp("row", [P, E + 2 * E * E + NT * E])
            eps_t = tmp("eps_t", [P, 1])
            stats = tmp("stats", [P, TT, 6])
            mv = tmp("mv", [P, TT, 2])
            std = tmp("std", [P, TT])
            rstd = tmp("rstd", [P, TT])
            shift = tmp("shift", [P, TT])
            coef_t = tmp("coef_t", [AUXP, 8])
            slope_in = tmp("slope_in", [AUXP, 2])
            sl = tmp("sl", [AUXP, 3, 2], BF16)
            slr = tmp("slr", [AUXP, 3, 2])
            cq = tmp("cq", [AUXP, 2, 2])
            prob = tmp("prob", [P, TT, E])
            biased = tmp("biased", [P, TT, E])
            rt = tmp("rt", [P, TT, E])
            pick = tmp("pick", [P, K_TOP, TT, E])
            picked = tmp("picked", [P, TT, E], BF16)
            top = tmp("top", [P, 8, TT])
            cnt = tmp("cnt", [P, 4, E])
            etab = tmp("etab", [P, NT * E])
            slot_f = tmp("slot_f", [P, K_TOP, TT])
            eid_f = tmp("eid_f", [P, NT])
            y_out = tmp("y_out", [P, 4, D])
            with ExitStack() as first:
                te_h = first.enter_context(nc.sbuf_tensor("te_h", [P, 2, F], F32))
                hh = first.enter_context(nc.sbuf_tensor("hh", [P, 2, F], F32))
            with nc.sbuf_tensor("logits_t", [E, T], F32) as logits_t:
                pass
            th = tmp("th", [P, 2, CH])
            hsh = tmp("hsh", [P, 2, CH])
            with ExitStack() as first:
                def now(name, shape, dt=F32):
                    return first.enter_context(nc.sbuf_tensor(name, shape, dt))

                w_nat = now("w_nat", [P, 6, D])
                wo_nat = now("wo_nat", [P, KC, H // HG, HG, 32])
                pos_t = now("pos_t", [AUXP, 2 * S], BF16)
                aux = now("aux", [AUXP, 4, S], BF16)
            w_dn = tmp("w_dn", [P, E, D])
            x_in = tmp("x_in", [P, 4, D])
            hx = tmp("hx", [P, 2, 1 + KC, P])
        pt = sb("pt", [P, 2, HG, CH])
        sums = sb("sums", [P, 3, NG, HG * S // P])
        sums_p = sb("sums_p", [P, 3, NG, HG * S // P], BF16)
        inv = sb("inv", [3 * HG, NG, S], BF16)
        ot = sb("ot", [P, NG, S])

        def bank(n, w=CH, m=P):
            return ps[0:m, n * CH:n * CH + w]

        idb = cbf[:, 0:P]
        mask_q = cbf[:, P:2 * P]
        mask_k = cbf[:, 2 * P:3 * P]

        qkd = nc.dram_tensor("qk_parts", [2, 3, NG, HD, HG, S], BF16, kind="Internal").ap()
        auxd = nc.dram_tensor("aux_rows", [2, NG, HG, N_AUX, S], BF16, kind="Internal").ap()
        xsd = nc.dram_tensor("sorted_tokens", [SLOTS, D], F32, kind="Internal").ap()
        ysd = nc.dram_tensor("sorted_outputs", [SLOTS, D], F32, kind="Internal").ap()

        s_x = [sem(f"x_loaded{i}") for i in range(4)]
        s_w = sem("w_loaded")
        s_c = sem("consts_loaded")
        s_wo = sem("wo_loaded")
        s_ws = sem("small_weights_loaded")
        s_wgu = sem("expert_gate_up_loaded")
        s_wdn = sem("expert_down_loaded")
        s_zero = sem("zeroed")
        s_clear = sem("slots_cleared")
        s_pool = sem("pool_step")
        s_ln = sem("statistics_ready")
        s_var = sem("variance_ready")
        s_std = sem("std_ready")
        s_shift = sem("shift_ready")
        s_rstd = sem("inverted_std_ready")
        s_qkb = sem("qk_bias_ready")
        s_small = sem("small_weights_high")
        s_smalll = sem("small_weights_low")
        s_xn = sem("tokens_normalised")
        s_xn2 = sem("last_tokens_normalised")
        s_job = sem("job_ready")
        s_hi = sem("hi_ready")
        s_free = sem("bank_freed")
        s_res = sem("parts_ready")
        s_mid = sem("mid_ready")
        s_parts = [sem(f"parts_stored{i}") for i in range(RING)]
        s_bias = sem("bias_permuted")
        s_id = sem("ident_loaded")
        s_aux = sem("aux_ready")
        s_auxst = sem("aux_stored")
        s_prob = sem("router_exp_ready")
        s_r = sem("router_step")
        s_picked = sem("picked_ready")
        s_rank = sem("ranks_ready")
        s_slot = sem("slots_ready")
        s_scat = sem("tokens_sorted")
        s_g1 = sem("shared_hidden_ready")
        s_th = sem("shared_tanh_ready")
        s_ta = sem("shared_step")
        s_h = sem("shared_h_ready")
        s_sh = sem("shared_out_ready")
        s_sha = sem("shared_added")
        s_xin = [sem(f"tile_loaded{i}") for i in range(4)]
        s_gu = sem("tile_gate_up_ready")
        s_tt = sem("tile_tanh_ready")
        s_tstep = sem("tile_step")
        s_hh = sem("tile_h_ready")
        s_hxt = sem("tile_transposed")
        s_hx = sem("tile_evacuated")
        s_dn = sem("tile_out_ready")
        s_yo = sem("tile_out_evacuated")
        s_ys = [sem(f"tile_out_stored{i}") for i in range(4)]
        s_ga = [sem(f"rows_gathered{i}") for i in range(4)]
        s_gw = sem("rows_weighed")
        s_gad = sem("rows_added")
        s_ld = [[[sem(f"{side}_half{half}_loaded{p}") for p in range(2)] for half in range(2)] for side in "qk"]
        s_first = [[[sem(f"first_{side}_half{half}_loaded{p}") for p in range(2)] for half in range(2)] for side in "qk"]
        s_vg = sem("vg_ready")
        s_fr = sem("first_max_scores_ready")
        s_ff = sem("first_max_scores_read")
        s_mxr = sem("max_scores_ready")
        s_mxf = sem("max_slot_freed")
        s_nstep = sem("neg_step")
        s_n = sem("neg_ready")
        s_nl = [sem(f"neg_loaded{p}") for p in range(2)]
        s_st = sem("scores_ready")
        s_exp = sem("exp_done")
        s_pv = sem("pv_done")
        s_ev = sem("out_evacuated")
        s_sums = [sem(f"sums_spread{i}") for i in range(3)]
        s_invs = sem("inversion_step")
        s_rec = sem("sums_inverted")
        s_invd = [sem(f"inverted_sums_in_rows{g}") for g in range(NG)]
        s_fin = sem("final_step_ready")
        s_inv = sem("final_bank_freed")
        s_y = sem("y_stored")

        block = ctx.enter_context(nc.Block())

        JOBS = ([("w", kc, c) for kc in range(KC) for c in range(3)] + [("x", n, 0) for n in range(TT // 2)]
                + [("b", 0, 0)] + [("o", oc, 0) for oc in range(2)] + [("g", n, 0) for n in range(T // CH)]
                + [("r", 0, 0)])
        for n in range(TT // 2):
            JOBS += [("qk", 2 * n % 4 + k, n // 2) for k in range(2)] + [("v", n, 0)]
        at = {kind: next(n for n, j in enumerate(JOBS) if j[0] == kind) for kind in ("x", "g")}
        X0, G0 = at["x"], at["g"]
        R0 = G0 + T // CH
        RANKS_AFTER = 7
        QKJ = [n for n, j in enumerate(JOBS) if j[0] == "qk"]
        NJ, NQK = len(JOBS), len(QKJ)
        HI_OF = [sum(j[0] in ("w", "x", "qk") for j in JOBS[:n + 1]) for n in range(NJ)]
        OUT_BANK = 3
        EXP_CREDIT, PV_CREDIT, MX_CREDIT = 3, 2, 2
        DMA = 16
        N_CONST = 10
        LOADS = 4
        SC = HD ** -0.5

        def load(queue, side, g, par, half, loaded):
            dst, order, done = (qs, ks)[side], (Q_PARTS, K_PARTS)[side], loaded[side][half][par]
            cols = slice(half * CH, (half + 1) * CH)
            for t0, n in ((0, 3), (3, 2), (5, 1)):
                p0 = order[t0]
                if side == 0:
                    src = qkd[0, p0:p0 + 1, bass.ds(g, 1), :, :, cols].rearrange("n g d j s -> (g n) d j s")
                    src = src.broadcast_to([n, HD, HG, CH])
                else:
                    src = qkd[1, 0:n, bass.ds(g, 1), :, :, cols].rearrange("n g d j s -> (g n) d j s")
                queue.dma_start(dst[HD * t0:HD * (t0 + n), par, :, cols], src).then_inc(done, DMA)
            rows = (N_ALIBI, N_AUX)[side]
            queue.dma_start(dst[AUX0:AUX0 + rows, par, :, cols],
                         auxd[side, bass.ds(g, 1), :, 0:rows, cols].rearrange("g j r s -> r (g j) s")
                         ).then_inc(done, DMA)

        @block.sync
        def _(sp):
            sp.dma_start(w_nat[:, :, :], qkv_w.rearrange("(c p) k -> p c k", p=P)).then_inc(s_w, DMA)
            xv = x.rearrange("b (t p) d -> p (b t) d", p=P)
            for n in range(4):
                sp.dma_start(x_sb[:, 4 * n:4 * n + 4, :], xv[:, 4 * n:4 * n + 4, :]).then_inc(s_x[n], DMA)
            for dst, src in ((cbf, c_bf), (pos_t, c_pos), (coef_t, c_coef), (sel, c_sel)):
                sp.dma_start(dst[:, :], src).then_inc(s_c, DMA)
            for half in range(2):
                heads = slopes[half * H // 2:(half + 1) * H // 2].rearrange("(h o) -> h o", o=1)
                sp.dma_start(slope_in[:, half:half + 1], heads.unsqueeze(1).broadcast_to([H // 2, N_AUX, 1])
                              ).then_inc(s_c, DMA)
            sp.dma_start(qkb_in[:, :], qkv_b[0:2 * D].rearrange("(c p) -> c p", p=P)).then_inc(s_c, DMA)
            sp.dma_start(vb[:, :], qkv_b[2 * D:3 * D].partition_broadcast(P)).then_inc(s_c, DMA)
            sp.dma_start(row[:, :], c_row.partition_broadcast(P)).then_inc(s_c, DMA)
            sp.dma_start(eb[:, :], ebias.partition_broadcast(P)).then_inc(s_c, DMA)
            sp.wait_ge(s_zero, 2)
            for oc in range(KC):
                sp.dma_start(wo_nat[:, oc, :, :, 0:HD].rearrange("p g j d -> p (g j) d"),
                              out_w[oc * P:(oc + 1) * P, :].rearrange("p (h d) -> p h d", d=HD)).then_inc(s_wo, DMA)
            sp.dma_start(wo_nat[:, :, 0, 0, HD:HD + 1].rearrange("p c o -> p (c o)"),
                          out_b.rearrange("(c p) -> p c", p=P), allow_slow_non_contiguous=True).then_inc(s_wo, DMA)
            sp.dma_start(wsd[:, :], sd_w).then_inc(s_wo, DMA)
            sp.wait_ge(s_zero, 3)
            sp.wait_ge(s_c, DMA * N_CONST)
            sp.wait_ge(s_wo, 4 * DMA)
            sp.wait_ge(s_ws, 3 * DMA)
            xz = xsd.rearrange("(p k) d -> p (k d)", p=P)
            for n in range(NT // 4):
                sp.dma_start(xz[:, n * 4 * D:(n + 1) * 4 * D], y_out[:, :, :].rearrange("p k d -> p (k d)")
                             ).then_inc(s_clear, DMA)
            for n in range(4):
                side, half = n // 2, n % 2
                sp.wait_ge(s_aux, n + 1)
                for b in range(B):
                    sp.dma_start(auxd[side, b * 4 + 2 * half:b * 4 + 2 * half + 2].rearrange("g j r s -> (g j r) s"),
                                 aux[:, n, :]).then_inc(s_auxst, DMA)
            sp.wait_ge(s_job, G0)
            sp.wait_ge(s_auxst, 4 * B * DMA)
            sp.dma_start(w_dn[:, :, :], e_dn.rearrange("e f d -> f e d")).then_inc(s_wdn, DMA)
            for i in range(NQK):
                _, fc, tc = JOBS[QKJ[i]]
                side, g0 = fc // 2, tc // 2 * 4 + fc % 2 * 2
                cols = slice(tc % 2 * CH, (tc % 2 + 1) * CH)
                sp.wait_ge(s_res, i + 1)
                sp.dma_start(qkd[side, :, g0:g0 + 2, :, :, cols].rearrange("n g d j s -> (g d j) n s"),
                             parts[:, i % RING, :, :]).then_inc(s_parts[i % RING], DMA)
            for i, stored in enumerate(s_parts):
                sp.wait_ge(stored, DMA * len(range(i, NQK, RING)))
            sp.dma_start(w_gu[:, :, :, :], e_gu.rearrange("e (c p) f -> p e c f", p=P)).then_inc(s_wgu, DMA)
            sp.wait_ge(s_scat, K_TOP * TT * DMA)

            def load_tile(k, u):
                sp.dma_start(x_in[:, u, :], xsd[bass.ds(k * P, P), :]).then_inc(s_xin[u], DMA)

            def store_tile(k, u):
                sp.wait_ge(s_yo, k + 1)
                sp.dma_start(ysd[bass.ds(k * P, P), :], y_out[:, u, :]).then_inc(s_ys[u], DMA)

            for k in range(4):
                load_tile(k, k)
            def store_neg(g, par):
                sp.wait_ge(s_n, g + 1)
                for r in range(3):
                    sp.dma_start(qs[N0 + r:N0 + r + 1, par, :, :].rearrange("o j (t c) -> o (j t) c", c=P),
                                 nr[:, par, r, :]).then_inc(s_nl[par], DMA)

            def next_tile(k, u):
                sp.wait_ge(s_hxt, k - 3)
                load_tile(k, u)

            for k in range(4, 7):
                next_tile(k, k % 4)
            with sp.Fori(0, NT // 4 - 2) as i:
                for u in range(4):
                    next_tile(i * 4 + u + 7, (u + 3) % 4)
                    store_tile(i * 4 + u, u)
            next_tile(NT - 1, 3)
            for k in range(NT - 8, NT):
                store_tile(k, k % 4)
            store_neg(0, 0)

            def group(g, par, ahead):
                if ahead >= 2:
                    sp.wait_ge(s_st, g * (HG * NS) + HG * 4)
                    load(sp, 0, g + 2, par, 0, s_ld)
                    sp.wait_ge(s_st, g * (HG * NS) + HG * 8)
                    load(sp, 1, g + 2, par, 0, s_ld)
                if ahead >= 1:
                    store_neg(g + 1, 1 - par)
                if ahead >= 2:
                    sp.wait_ge(s_st, g * (HG * NS) + HG * NS)
                    load(sp, 0, g + 2, par, 1, s_ld)
                    load(sp, 1, g + 2, par, 1, s_ld)

            with sp.Fori(0, NG // 2 - 1) as i:
                group(i * 2, 0, 2)
                group(i * 2 + 1, 1, 2)
            group(NG - 2, 0, 1)
            for g in range(NG):
                sp.wait_ge(s_rec, max(0, g - (NG - 3)) + 1)
                for k in range(3):
                    sp.dma_start(inv[HG * k:HG * (k + 1), g, :].rearrange("j (c s) -> j c s", s=HG * S // P),
                                 sums_p[:, k, g, :]).then_inc(s_invd[g], DMA)
            yv = y.rearrange("b (t p) d -> p (b t) d", p=P)
            for t in range(TT):
                sp.wait_ge(s_inv, FINAL.index(("project", t)) + 1)
                sp.dma_start(yv[:, t, :], x_sb[:, t, :]).then_inc(s_y, DMA)
            sp.wait_ge(s_y, DMA * TT)

        @block.gpsimd
        def _(pool):
            g_ = nc.gpsimd
            step = [0]

            def link(ins):
                ins.then_inc(s_pool, 1)
                step[0] += 1
                pool.wait_ge(s_pool, step[0])

            g_.memset(y_out[:, :, :], 0.0).then_inc(s_zero, 1)
            g_.memset(wo_nat[:, :, :, :, :], 0.0).then_inc(s_zero, 1)
            g_.memset(eps_t[:, :], LN_EPS).then_inc(s_zero, 1)
            g_.memset(mv_pad[:, 0:1], 0.0).then_inc(s_pv, PV_CREDIT)
            g_.memset(mv_pad[:, 1:2], 0.0).then_inc(s_ev, 1)
            for n in range(8):
                g_.memset(mv_pad[:, 3 + n:4 + n], 0.0).then_inc(s_ld[n // 4][n // 2 % 2][n % 2], LOADS * DMA)
            link(g_.memset(vg[:, :, :, :, :], 0.0))
            link(g_.memset(vg[:, :, :, :, HD:HD + 1], 1.0))
            pool.wait_ge(s_c, DMA * N_CONST)
            g_.tensor_copy(qkb_row[:, :].rearrange("p (g d j) -> p g j d", j=HG, d=HD),
                           qkb_in[:, :].rearrange("p (g j d) -> p g j d", j=HG, d=HD)).then_inc(s_bias, 1)
            link(g_.tensor_copy(sl[:, 0, :], slope_in[:, :]))
            link(g_.tensor_tensor(slr[:, 1, :], slope_in[:, :], sl[:, 0, :], ALU.subtract))
            link(g_.tensor_copy(sl[:, 1, :], slr[:, 1, :]))
            link(g_.tensor_tensor(slr[:, 2, :], slr[:, 1, :], sl[:, 1, :], ALU.subtract))
            link(g_.tensor_copy(sl[:, 2, :], slr[:, 2, :]))
            for side in range(2):
                c = coef_t[:, 4 * side:4 * side + 4]
                link(g_.tensor_scalar(cq[:, side, :], sl[:, 0, :], c[:, 0:1], c[:, 3:4], ALU.mult, ALU.add))
                for k in (1, 2):
                    link(g_.tensor_scalar(slr[:, 0, :], sl[:, k, :], c[:, k:k + 1], None, ALU.mult))
                    link(g_.tensor_tensor(cq[:, side, :], cq[:, side, :], slr[:, 0, :], ALU.add))
            for n in range(4):
                side, half = n // 2, n % 2
                g_.tensor_scalar(aux[:, n, :], pos_t[:, side * S:(side + 1) * S], cq[:, side, half:half + 1], None,
                                ALU.mult).then_inc(s_aux, 1)
            pool.wait_ge(s_slot, 1)
            pool.wait_ge(s_clear, NT // 4 * DMA)
            for t in range(TT):
                for k in range(K_TOP):
                    g_.indirect_dma_start(out=xsd, out_offset=bass.IndirectOffsetOnAxis(ap=slot_i[:, k, t:t + 1], axis=0),
                                          in_=xn[:, t, :], in_offset=None).then_inc(s_scat, DMA)

            def copy_v(g, par):
                g_.tensor_copy(vg[:, par, :, :, 0:HD],
                               v_sb[:, bass.ds(g, 1), :, :].rearrange("p g t (j d) -> p (g t) j d", d=HD)
                               ).then_inc(s_vg, 1)

            pool.wait_ge(s_free, NJ)
            copy_v(0, 0)
            copy_v(1, 1)
            pool.wait_ge(s_sh, TT // 2)
            for i, stored in enumerate(s_parts):
                pool.wait_ge(stored, DMA * len(range(i, NQK, RING)))
            for g in range(2):
                for half in range(2):
                    load(pool, 0, g, g, half, s_first)
                    load(pool, 1, g, g, half, s_first)
            for u in range(4):
                pool.wait_ge(s_ys[u], NT // 4 * DMA)
            pool.wait_ge(s_sha, TT // 2)

            def copy_next(i, par):
                pool.wait_ge(s_pv, PV_CREDIT + i * (2 * NS) + NS * (par + 1))
                copy_v(i * 2 + par + 2, par)

            def gather(n):
                t, k = n // K_TOP, n % K_TOP
                g_.indirect_dma_start(out=yg[:, n % 4, :], out_offset=None, in_=ysd,
                                      in_offset=bass.IndirectOffsetOnAxis(ap=slot_i[:, k, t:t + 1], axis=0)
                                      ).then_inc(s_ga[n % 4], DMA)

            for n in range(3):
                gather(n)
            for n in range(K_TOP * TT):
                if n == K_TOP * TT // 2:
                    copy_next(0, 0)
                if n + 3 < K_TOP * TT:
                    if n >= 1:
                        pool.wait_ge(s_gad, n)
                    gather(n + 3)
                t, k = n // K_TOP, n % K_TOP
                pool.wait_ge(s_ga[n % 4], DMA * (n // 4 + 1))
                g_.tensor_scalar(yg[:, n % 4, :], yg[:, n % 4, :], gates[:, k, t:t + 1], None, ALU.mult
                                 ).then_inc(s_gw, 1)
                pool.wait_ge(s_gw, n + 1)
                if n >= 1:
                    pool.wait_ge(s_gad, n)
                g_.tensor_tensor(x_sb[:, t, :], x_sb[:, t, :], yg[:, n % 4, :], ALU.add).then_inc(s_gad, 1)
            def spread_sums(g, spread):
                pool.wait_ge(s_ev, g * 2 + 3)
                pool.dma_start(sums[:, 0, bass.ds(g, 1), :].rearrange("p g s -> p (g s)"),
                               ot[HD::32, bass.ds(g, 1), :].rearrange("j g (c s) -> j (g c) s", s=HG * S // P)
                               ).then_inc(spread, DMA)

            copy_next(0, 1)
            for g in range(2):
                spread_sums(g, s_sums[0])
            with pool.Fori(1, NG // 2 - 1) as i:
                for par in range(2):
                    copy_next(i, par)
                    spread_sums(i * 2 + par, s_sums[0])
            for g in range(NG - 2, NG):
                spread_sums(g, s_sums[g - (NG - 3)])

        @block.scalar
        def _(act):
            sc = nc.scalar
            act.dma_start(ident[:, :], c_ident).then_inc(s_id, DMA)
            act.dma_start(perm[:, :], c_perm).then_inc(s_id, DMA)
            act.dma_start(gw[:, :, :], gate_w.rearrange("(c p) e -> p c e", p=P)).then_inc(s_ws, DMA)
            act.dma_start(ws[:, :, 0, :], sg_w.rearrange("(c p) f -> p c f", p=P)).then_inc(s_ws, DMA)
            act.dma_start(ws[:, :, 1, :], su_w.rearrange("(c p) f -> p c f", p=P)).then_inc(s_ws, DMA)

            def high(n):
                kind, a, b = JOBS[n]
                src = bank(n % 8)
                if kind in ("w", "x", "qk", "r"):
                    act.wait_ge(s_job, n + 1)
                if kind == "w":
                    sc.activation(wh[:, a, b * D:(b + 1) * D], src[:, 0:D], ACT.Copy,
                                  scale=SC if b == 0 else 1.0).then_inc(s_hi, 1)
                elif kind == "x":
                    dst = xh[:, :, 2 * a * P:(2 * a + 2) * P].rearrange("p c (t n) -> p t c n", n=P)
                    sc.activation(dst, src.rearrange("p (t c n) -> p t c n", t=2, c=KC), ACT.Copy).then_inc(s_hi, 1)
                elif kind == "r":
                    sc.activation(prob[:, :, :], src[:, 0:TT * E].rearrange("p (t e) -> p t e", e=E), ACT.Exp,
                                  scale=-1.0).then_inc(s_prob, 1)
                elif kind == "qk":
                    i = QKJ.index(n)
                    if i == 0:
                        act.wait_ge(s_qkb, 2)
                    if i >= RING:
                        act.wait_ge(s_parts[i % RING], DMA * (i // RING))
                    sc.activation(parts[:, i % RING, 0, :], src, ACT.Identity, bias=qkb[:, a:a + 1]).then_inc(s_hi, 1)
                    if i:
                        middle(i - 1)

            def middle(i):
                act.wait_ge(s_free, QKJ[i] + 1)
                sc.activation(parts[:, i % RING, 1, :], part_r[:, i % RING, :], ACT.Copy).then_inc(s_mid, 1)

            act.wait_ge(s_zero, 3)
            for q in range(4):
                act.wait_ge(s_var, 4 * q + 4)
                sc.activation(std[:, 4 * q:4 * q + 4], mv[:, 4 * q:4 * q + 4, 1], ACT.Sqrt, bias=eps_t[:, :]
                              ).then_inc(s_std, 1)
                if q == 0:
                    for n in range(X0):
                        high(n)
            for q in (2, 3):
                act.wait_ge(s_shift, q - 1)
                for t in range(4 * q, 4 * q + 4):
                    sc.activation(xn[:, t, :], x_sb[:, t, :], ACT.Identity, bias=shift[:, t:t + 1],
                                  scale=rstd[:, t:t + 1]).then_inc(s_xn2, 1)
            act.wait_ge(s_ws, 3 * DMA)
            sc.activation(gwh[:, :, :], gw[:, :, :], ACT.Copy).then_inc(s_small, 1)
            sc.activation(wsh[:, :, :, :], ws[:, :, :, :], ACT.Copy).then_inc(s_small, 1)
            for n in range(X0, G0):
                high(n)
            for n in range(G0, NJ):
                high(n)
            middle(NQK - 1)
            for c in range(4):
                act.wait_ge(s_g1, c + 1)
                if c >= 2:
                    act.wait_ge(s_h, c - 1)
                sc.activation(th[:, c % 2, :], bank(2 * c), ACT.Tanh, scale=0.5).then_inc(s_th, 1)

            def evacuate_tokens(k):
                act.wait_ge(s_hxt, k + 1)
                sc.activation(hx[:, (k + 1) % 2, 1:, :], bank((k + 1) % 2)[:, P:(1 + KC) * P].rearrange(
                    "p (c n) -> p c n", n=P), ACT.Copy).then_inc(s_hx, 1)

            def tile_tanh(k, v):
                act.wait_ge(s_gu, k + 1)
                sc.activation(te_h[:, v, :], bank(2 + v, F), ACT.Tanh, scale=0.5).then_inc(s_tt, 1)

            def tile_step(k, u, left):
                act.wait_ge(s_hxt, k + 4)
                c1 = 1 + KC if left > 3 else 1
                sc.activation(hx[:, u % 2, 0:c1, :], bank(u % 2)[:, 0:c1 * P].rearrange("p (c n) -> p c n", n=P),
                              ACT.Copy).then_inc(s_hx, 1)
                if left > 2:
                    tile_tanh(k + 2, u % 2)

            for k in range(2):
                evacuate_tokens(k)
            for k in range(2):
                tile_tanh(k, k)
            evacuate_tokens(2)
            with act.Fori(0, HG - 1) as j:
                for u in range(NTH):
                    tile_step(j * NTH + u, u, NT)
            for u in range(NTH):
                tile_step(NT - NTH + u, u, NTH - u)
            sc.activation(std[:, 0:1], std[:, 1:2], ACT.Exp).then_inc(s_exp, EXP_CREDIT)

            def exps(g, s, par):
                qc, kb = STEPS[s]
                lo = max(0, kb * P - qc * CH)
                for j in range(HG):
                    n = HG * s + j
                    act.wait_ge(s_st, g * (HG * NS) + n + 1)
                    if j == 0:
                        act.wait_ge(s_pv, g * NS + s + 1)
                    sc.activation(pt[:, s % 2, j, lo:CH], bank(n % 3)[:, lo:CH], ACT.Exp).then_inc(s_exp, 1)

            def evacuate(g, qc):
                act.wait_ge(s_pv, PV_CREDIT + g * NS + (4 if qc == 0 else NS))
                sc.activation(ot[:, bass.ds(g, 1), qc * CH:(qc + 1) * CH].rearrange("p g s -> p (g s)"),
                              bank(OUT_BANK), ACT.Copy).then_inc(s_ev, 1)

            def pair(g):
                for s in range(2 * NS):
                    par, st = s // NS, s % NS
                    exps(g + par, st, par)
                    if st == 4:
                        evacuate(g + par, 0)
                    if s == NS:
                        evacuate(g, 1)
                evacuate(g + 1, 1)

            with act.Fori(0, NG // 2 - 1) as i:
                pair(i * 2)
            pair(NG - 2)

        @block.vector
        def _(dve):
            v = nc.vector
            v.memset(mx[:, :, :], 0.0).then_inc(s_mxf, MX_CREDIT)
            def statistics(q):
                dve.wait_ge(s_x[q], DMA)
                for t in range(4 * q, 4 * q + 4):
                    v.bn_stats(stats[:, t, :], x_sb[:, t, :]).then_inc(s_ln, 1)
                for t in range(4 * q, 4 * q + 4):
                    dve.wait_ge(s_ln, t + 1)
                    v.bn_aggr(mv[:, t, :], stats[:, t, :]).then_inc(s_var, 1)

            def normalise(q):
                dve.wait_ge(s_std, q + 1)
                v.reciprocal(rstd[:, 4 * q:4 * q + 4], std[:, 4 * q:4 * q + 4]).then_inc(s_rstd, 1)
                dve.wait_ge(s_rstd, q + 1)
                if q >= 2:
                    v.scalar_tensor_tensor(shift[:, 4 * q:4 * q + 4], mv[:, 4 * q:4 * q + 4, 0], -1.0,
                                           rstd[:, 4 * q:4 * q + 4], ALU.mult, ALU.mult).then_inc(s_shift, 1)
                    return
                for t in range(4 * q, 4 * q + 4):
                    v.tensor_scalar(xn[:, t, :], x_sb[:, t, :], mv[:, t, 0:1], rstd[:, t:t + 1],
                                    ALU.subtract, ALU.mult).then_inc(s_xn, 1)

            def last_part(i):
                dve.wait_ge(s_mid, i + 1)
                v.tensor_tensor(parts[:, i % RING, 2, :], part_r[:, i % RING, :], parts[:, i % RING, 1, :],
                                ALU.subtract).then_inc(s_res, 1)

            def low(n):
                kind, a, b = JOBS[n]
                dve.wait_ge(s_job, n + 1)
                src = bank(n % 8)
                if kind == "w":
                    dve.wait_ge(s_hi, HI_OF[n])
                    v.scalar_tensor_tensor(wl[:, a, b * D:(b + 1) * D], src[:, 0:D], SC if b == 0 else 1.0,
                                           wh[:, a, b * D:(b + 1) * D], ALU.mult, ALU.subtract).then_inc(s_free, 1)
                elif kind == "o":
                    v.tensor_copy(wo_t[:, :, a * P:(a + 1) * P],
                                  src.rearrange("p (g n) -> p g n", n=P)).then_inc(s_free, 1)
                elif kind == "b":
                    v.tensor_scalar(qkb[:, 0:2], src[:, 0:2], SC, None, ALU.mult).then_inc(s_qkb, 1)
                    v.tensor_copy(qkb[:, 2:4], src[:, 2:4]).then_inc(s_qkb, 1)
                    dve.wait_ge(s_qkb, 2)
                    v.memset(mv_pad[:, 2:3], 0.0).then_inc(s_free, 1)
                elif kind == "x":
                    dve.wait_ge(s_hi, HI_OF[n])
                    cols = slice(2 * a * P, (2 * a + 2) * P)
                    v.tensor_tensor(xl[:, :, cols].rearrange("p c (t n) -> p t c n", n=P),
                                    src.rearrange("p (t c n) -> p t c n", t=2, c=KC),
                                    xh[:, :, cols].rearrange("p c (t n) -> p t c n", n=P),
                                    ALU.subtract).then_inc(s_free, 1)
                elif kind == "g":
                    v.tensor_copy(logits_t[:, a * CH:(a + 1) * CH], src[0:E, :]).then_inc(s_free, 1)
                elif kind == "r":
                    route()
                    place()
                elif kind == "qk":
                    i = QKJ.index(n)
                    dve.wait_ge(s_hi, HI_OF[n])
                    v.scalar_tensor_tensor(part_r[:, i % RING, :], src, qkb[:, a:a + 1], parts[:, i % RING, 0, :],
                                           ALU.add, ALU.subtract).then_inc(s_free, 1)
                    if i:
                        last_part(i - 1)
                else:
                    t = 2 * a
                    b_, kb = t // QT, t % QT
                    dst = v_sb[:, 4 * b_:4 * b_ + 4, kb:kb + 2, :].rearrange("p g t n -> p t g n")
                    v.tensor_tensor(dst, src.rearrange("p (t g n) -> p t g n", t=2, g=4),
                                    vb[:, :].rearrange("p (o g n) -> p o g n", o=1, g=4).to_broadcast([P, 2, 4, HG * HD]),
                                    ALU.add).then_inc(s_free, 1)

            steps = [0]

            def then(ins):
                ins.then_inc(s_r, 1)
                steps[0] += 1
                dve.wait_ge(s_r, steps[0])

            def over_e(ap):
                return ap.unsqueeze(2).broadcast_to([P, TT, E])

            def over_t(ap):
                return ap.unsqueeze(1).broadcast_to([P, TT, E])

            rank_row = row[:, 0:E]
            before = row[:, E:E + E * E].rearrange("p (a b) -> p a b", b=E)
            fills = row[:, E + E * E:E + 2 * E * E].rearrange("p (a b) -> p a b", b=E)
            tile_no = row[:, E + 2 * E * E:].rearrange("p (k e) -> p k e", e=E)

            def route():
                dve.wait_ge(s_prob, 1)
                then(v.tensor_scalar(rt[:, :, :], prob[:, :, :], 1.0, None, ALU.add))
                then(v.reciprocal(prob[:, :, :], rt[:, :, :]))
                then(v.tensor_tensor(biased[:, :, :], prob[:, :, :], over_t(eb[:, :]), ALU.add))
                for k in range(K_TOP):
                    p_ = pick[:, k, :, :]
                    then(v.reduce_max(top[:, 0, :], biased[:, :, :], axis=AX.X))
                    then(v.tensor_tensor(rt[:, :, :], biased[:, :, :], over_e(top[:, 0, :]), ALU.is_equal))
                    then(v.tensor_tensor(rt[:, :, :], rt[:, :, :], over_t(rank_row), ALU.mult))
                    then(v.reduce_max(top[:, 1, :], rt[:, :, :], axis=AX.X))
                    then(v.tensor_tensor(p_, rt[:, :, :], over_e(top[:, 1, :]), ALU.is_equal))
                    if k == 0:
                        then(v.scalar_tensor_tensor(biased[:, :, :], p_, NEG, biased[:, :, :], ALU.mult, ALU.add))
                v.tensor_tensor(picked[:, :, :], pick[:, 0, :, :], pick[:, 1, :, :], ALU.add).then_inc(s_picked, 1)
                for k in range(K_TOP):
                    then(v.tensor_tensor(rt[:, :, :], pick[:, k, :, :], prob[:, :, :], ALU.mult))
                    then(v.reduce_sum(top[:, 2 + k, :], rt[:, :, :], axis=AX.X))
                then(v.scalar_tensor_tensor(top[:, 4, :], top[:, 2, :], 1e-20, top[:, 3, :], ALU.add, ALU.add))
                then(v.reciprocal(top[:, 5, :], top[:, 4, :]))
                for k in range(K_TOP):
                    then(v.tensor_tensor(gates[:, k, :], top[:, 2 + k, :], top[:, 5, :], ALU.mult))

            def place():
                dve.wait_ge(s_rank, 1)
                ranks = bank(R0 % 8)
                counts = ranks[:, TT * E:TT * E + E]
                sq = [P, E, E]
                then(v.tensor_tensor(rt[:, :, :], counts.unsqueeze(2).broadcast_to(sq), fills, ALU.is_gt))
                then(v.reduce_sum(cnt[:, 0, :], rt[:, :, :], axis=AX.X))
                then(v.tensor_tensor(rt[:, :, :], cnt[:, 0, :].unsqueeze(1).broadcast_to(sq), before, ALU.mult))
                then(v.reduce_sum(cnt[:, 1, :], rt[:, :, :], axis=AX.X))
                then(v.tensor_tensor(cnt[:, 2, :], cnt[:, 0, :], cnt[:, 1, :], ALU.add))
                then(v.tensor_scalar(cnt[:, 3, :], cnt[:, 1, :], float(P), None, ALU.mult))
                then(v.tensor_tensor(rt[:, :, :], ranks[:, 0:TT * E].rearrange("p (t e) -> p t e", e=E),
                                     over_t(cnt[:, 3, :]), ALU.add))
                for k in range(K_TOP):
                    then(v.tensor_tensor(biased[:, :, :], pick[:, k, :, :], rt[:, :, :], ALU.mult))
                    then(v.reduce_sum(slot_f[:, k, :], biased[:, :, :], axis=AX.X))
                v.tensor_copy(slot_i[:, :, :], slot_f[:, :, :]).then_inc(s_slot, 1)
                et = etab[:, :].rearrange("p (k e) -> p k e", e=E)
                then(v.tensor_tensor(et, cnt[:, 2, :].unsqueeze(1).broadcast_to([P, NT, E]), tile_no, ALU.is_le))
                then(v.reduce_sum(eid_f[:, :], et, axis=AX.X))
                v.tensor_scalar(eid[:, :], eid_f[:, :], float(E - 1), None, ALU.min).then_inc(s_free, 1)

            for q in range(4):
                statistics(q)
                if q in (1, 2):
                    normalise(q - 1)
            for q in (2, 3):
                normalise(q)
            for n in range(X0):
                low(n)
            dve.wait_ge(s_small, 2)
            v.tensor_tensor(gwl[:, :, :], gw[:, :, :], gwh[:, :, :], ALU.subtract).then_inc(s_smalll, 1)
            v.tensor_tensor(wsl[:, :, :, :], ws[:, :, :, :], wsh[:, :, :, :], ALU.subtract).then_inc(s_smalll, 1)
            for n in range(X0, G0):
                low(n)
            for n in range(G0, NJ):
                low(n)
                if n == QKJ[-1]:
                    last_part(NQK - 1)
            def add_shared(n):
                dve.wait_ge(s_sh, n + 1)
                xs = x_sb[:, 2 * n:2 * n + 2, :].rearrange("p t d -> p (t d)")
                v.tensor_tensor(xs, xs, bank(n), ALU.add).then_inc(s_sha, 1)

            for c in range(4):
                dve.wait_ge(s_th, c + 1)
                v.scalar_tensor_tensor(th[:, c % 2, :], th[:, c % 2, :], 1.0, bank(2 * c), ALU.add, ALU.mult
                                       ).then_inc(s_ta, 1)
                dve.wait_ge(s_ta, c + 1)
                if c >= 2:
                    dve.wait_ge(s_sh, 2 * (c - 1))
                v.scalar_tensor_tensor(hsh[:, c % 2, :], th[:, c % 2, :], 0.5, bank(2 * c + 1), ALU.mult, ALU.mult
                                       ).then_inc(s_h, 1)
                if c >= 2:
                    for n in range(2 * (c - 2), 2 * (c - 1)):
                        add_shared(n)
            for n in range(TT // 4, TT // 2):
                add_shared(n)

            def tile_hidden(k, w):
                dve.wait_ge(s_tt, k + 1)
                v.scalar_tensor_tensor(te_h[:, w, :], te_h[:, w, :], 1.0, bank(2 + w, F), ALU.add, ALU.mult
                                       ).then_inc(s_tstep, 1)
                dve.wait_ge(s_tstep, k + 1)
                v.scalar_tensor_tensor(hh[:, w, :], te_h[:, w, :], 0.5, ps[:, (2 + w) * CH + F:(2 + w) * CH + 2 * F],
                                       ALU.mult, ALU.mult).then_inc(s_hh, 1)

            def tile_step(k, u, left, stored):
                dve.wait_ge(s_dn, k + 1)
                if stored is not None:
                    dve.wait_ge(s_ys[u], stored)
                v.tensor_copy(y_out[:, u, :], bank(4 + u % 2, D)).then_inc(s_yo, 1)
                if left > 2:
                    tile_hidden(k + 2, u % 2)

            def first_maxima(j, q, n):
                dve.wait_ge(s_fr, n + 1)
                v.reduce_max(mx[:, 0, :].rearrange("p (j t) -> p j t", j=HG)[:, bass.ds(j, 1), q],
                             ps[:, 6 * CH:6 * CH + (q + 1) * P], axis=AX.X).then_inc(s_ff, 1)

            def tile_steps(j, last):
                k = j * NTH
                for u in range(NTH):
                    tile_step(k + u, u % 4, NTH - u if last else NT, None if u < 4 and type(j) is int and j == 0 else (j * (NTH // 4) + u // 4) * DMA)
                    for q in range(QT):
                        if FIRST_AT[q] == u:
                            first_maxima(j, q, j * QT + q)

            for k in range(2):
                tile_hidden(k, k)
            tile_steps(0, False)
            with dve.Fori(1, HG - 1) as j:
                tile_steps(j, False)
            tile_steps(HG - 1, True)

            def maxima(g, par, p):
                n = (g - 1) * NP + p
                qt, j0, nj = PIECES[p]
                w = (qt + 1) * P
                dve.wait_ge(s_mxr, n + 1)
                src = ps[:, (4 + 2 * (p % 2)) * CH:(4 + 2 * (p % 2)) * CH + nj * w].rearrange("p (j w) -> p j w", j=nj)
                dst = mx[:, par, :].rearrange("p (j t) -> p j t", j=HG)[:, j0:j0 + nj, qt]
                last = v.reduce_max(dst, src, axis=AX.X)
                last.then_inc(s_mxf, 1)

            def negate(g, par, first=False):
                ready, freed, n = (s_fr, s_ff, HG * QT) if first else (s_mxr, s_mxf, g * NP - 1)
                dve.wait_ge(ready, n + 1)
                src = bank(6, P, HG * QT)
                v.tensor_scalar(nr[:, par, 0, :], src, -1.0, None, ALU.mult).then_inc(s_nstep, 1)
                dve.wait_ge(s_nstep, g * 2 + 1)
                v.scalar_tensor_tensor(nrf[:, par, :], src, -1.0, nr[:, par, 0, :], ALU.mult,
                                       ALU.subtract).then_inc(freed, 1)
                dve.wait_ge(freed, n + 1 if first else MX_CREDIT + n + 1)
                v.tensor_copy(nr[:, par, 1, :], nrf[:, par, :]).then_inc(s_nstep, 1)
                dve.wait_ge(s_nstep, g * 2 + 2)
                v.tensor_tensor(nr[:, par, 2, :], nrf[:, par, :], nr[:, par, 1, :], ALU.subtract).then_inc(s_n, 1)

            def beside(g, par, ahead):
                for dg, p in [x[1:] for x in ORDER if x[0] == "max"]:
                    if dg > ahead:
                        continue
                    q = (par + dg) % 2
                    if p == NP - 1:
                        negate(g + dg, q)
                    else:
                        maxima(g + dg, q, p)

            negate(0, 0, first=True)
            for p in range(EARLY):
                maxima(1, 1, p)

            with dve.Fori(0, NG // 2 - 1) as i:
                for par in range(2):
                    beside(i * 2 + par, par, 2)
            beside(NG - 2, 0, 1)
            inverted = [0]

            def inverting(ins):
                ins.then_inc(s_invs, 1)
                inverted[0] += 1
                dve.wait_ge(s_invs, inverted[0])

            def invert(g0, g1):
                dve.wait_ge(s_sums[max(0, g0 - (NG - 3))], (g1 - g0) * DMA)
                whole, rest, part = sums[:, 1, g0:g1, :], sums[:, 2, g0:g1, :], sums_p[:, :, g0:g1, :]
                inverting(v.reciprocal(whole, sums[:, 0, g0:g1, :]))
                inverting(v.tensor_copy(part[:, 0], whole))
                inverting(v.tensor_tensor(rest, whole, part[:, 0], ALU.subtract))
                inverting(v.tensor_copy(part[:, 1], rest))
                v.tensor_tensor(part[:, 2], rest, part[:, 1], ALU.subtract).then_inc(s_rec, 1)

            invert(0, NG - 2)
            invert(NG - 2, NG - 1)
            dve.wait_ge(s_gad, K_TOP * TT)
            for m, (kind, n) in enumerate(FINAL):
                if m == SUMS_AT:
                    invert(NG - 1, NG)
                dve.wait_ge(s_fin, m + 1)
                if kind == "divide":
                    o = ot[:, n // 2, n % 2 * CH:(n % 2 + 1) * CH]
                    v.tensor_tensor(o, o, bank(4 + m % 4), ALU.mult).then_inc(s_inv, 1)
                else:
                    v.tensor_tensor(x_sb[:, n, :], x_sb[:, n, :], bank(4 + m % 4, D), ALU.add).then_inc(s_inv, 1)

        @block.tensor
        def _(pe):
            te = nc.tensor

            def split_product(out, sides, first=True, last=True):
                ops = [(l, r) for (ah, al, bh, bl) in sides for l, r in ((al, bh), (ah, bl), (ah, bh))]
                for k, (l, r) in enumerate(ops):
                    ins = te.matmul(out, l, r, start=k == 0, stop=k == len(ops) - 1)
                return ins

            def rank():
                ranks = bank(R0 % 8)
                pe.wait_ge(s_c, DMA * N_CONST)
                pe.wait_ge(s_picked, 1)
                for t in range(TT):
                    te.matmul(ranks[:, TT * E:TT * E + E], cbf[:, 4 * P:5 * P], picked[:, t, :],
                              start=t == 0, stop=t == TT - 1)
                te.matmul(ranks[:, 0:TT * E], cbf[:, 3 * P:4 * P], picked[:, :, :].rearrange("p t e -> p (t e)"),
                          start=True, stop=False)
                for t in range(TT - 1):
                    ins = te.matmul(ranks[:, (t + 1) * E:TT * E], cbf[:, 4 * P:5 * P],
                                    picked[:, t, :].unsqueeze(1).broadcast_to([P, TT - 1 - t, E]),
                                    start=False, stop=t == TT - 2)
                ins.then_inc(s_rank, 1)

            pe.wait_ge(s_id, 2 * DMA)
            for n, (kind, a, b) in enumerate(JOBS):
                out = bank(n % 8)
                if n >= 8:
                    pe.wait_ge(s_free, n - 7)
                if kind == "w":
                    pe.wait_ge(s_w, DMA)
                    for k in range(2):
                        ins = te.matmul(out[:, k * P:(k + 1) * P], w_nat[:, 2 * b + k, a * P:(a + 1) * P],
                                        (perm, perm, ident)[b][:, :], start=True, stop=True)
                elif kind == "o":
                    pe.wait_ge(s_wo, 4 * DMA)
                    for hg in range(H // HG):
                        ins = te.transpose(out[:, hg * P:(hg + 1) * P],
                                           wo_nat[:, a, hg, :, :].rearrange("p j d -> p (j d)"), ident[:, :])
                elif kind == "b":
                    pe.wait_ge(s_bias, 1)
                    ins = te.transpose(out[:, 0:4], qkb_row[:, :], ident[0:4, 0:4])
                elif kind == "x":
                    pe.wait_ge((s_xn, s_xn2)[a // 4], 2 * (a % 4) + 2)
                    for k in range(4):
                        ins = te.transpose(out[:, k * P:(k + 1) * P],
                                           xn[:, 2 * a + k // 2, k % 2 * P:(k % 2 + 1) * P], ident[:, :])
                elif kind == "g":
                    pe.wait_ge(s_free, X0 + 2 * a + 2)
                    pe.wait_ge(s_smalll, 2)
                    ts = slice(a * CH, (a + 1) * CH)
                    ops = [(l, r) for c in range(KC)
                           for l, r in ((gwl[:, c, :], xl[:, c, ts]), (gwh[:, c, :], xl[:, c, ts]),
                                        (gwl[:, c, :], xh[:, c, ts]), (gwh[:, c, :], xh[:, c, ts]))]
                    for k, (l, r) in enumerate(ops):
                        ins = te.matmul(out[0:E, :], l, r, start=k == 0, stop=k == len(ops) - 1)
                elif kind == "r":
                    pe.wait_ge(s_free, n)
                    for t in range(TT):
                        ins = te.transpose(out[:, t * E:(t + 1) * E], logits_t[:, t * P:(t + 1) * P],
                                           ident[0:E, 0:E])
                elif kind == "qk":
                    f, t = slice(a * P, (a + 1) * P), slice(b * CH, (b + 1) * CH)
                    ins = split_product(out, [(wh[:, c, f], wl[:, c, f], xh[:, c, t], xl[:, c, t]) for c in range(KC)])
                else:
                    w = slice(2 * D, 3 * D)
                    for k in range(2):
                        t = slice((2 * a + k) * P, (2 * a + k + 1) * P)
                        ins = split_product(out[:, k * D:(k + 1) * D],
                                            [(xh[:, c, t], xl[:, c, t], wh[:, c, w], wl[:, c, w]) for c in range(KC)])
                ins.then_inc(s_job, 1)
                if n == R0 + RANKS_AFTER:
                    rank()

            def shared_down(c):
                pe.wait_ge(s_h, c + 1)
                for t in range(4):
                    ins = te.matmul(ps[:, 2 * c * CH + t * D:2 * c * CH + (t + 1) * D],
                                    hsh[:, c % 2, t * P:(t + 1) * P], wsd[:, :], start=True, stop=True)
                    if t % 2:
                        ins.then_inc(s_sh, 1)

            for c in range(4):
                t = slice(c * CH, (c + 1) * CH)
                pe.wait_ge(s_free, max(n for n in range(NJ) if n % 8 in (2 * c, 2 * c + 1)) + 1)
                for k in range(2):
                    ins = split_product(bank(2 * c + k), [(wsh[:, m, k, :], wsl[:, m, k, :], xh[:, m, t], xl[:, m, t])
                                                          for m in range(KC)])
                ins.then_inc(s_g1, 1)
                if c:
                    shared_down(c - 1)
            shared_down(3)

            def tokens_in(k, u, v, need):
                pe.wait_ge(s_xin[u], need)
                for c in range(KC):
                    ins = te.transpose(ps[:, v * CH + (1 + c) * P:v * CH + (2 + c) * P],
                                       x_in[:, u, c * P:(c + 1) * P], ident[:, :])
                return ins

            def expert_of(k):
                return pe.value_load(eid[0:1, bass.ds(k, 1)], min_val=0, max_val=E - 1)

            def gate_up(k, w):
                e = expert_of(k)
                for c in range(KC):
                    ins = te.matmul(bank(2 + w, 2 * F), hx[:, 1 - w, 1 + c, :],
                                    w_gu[:, bass.ds(e, 1), c, :].rearrange("p o f -> p (o f)"),
                                    start=c == 0, stop=c == KC - 1)
                ins.then_inc(s_gu, 1)

            def tile_step(k, u, left, need):
                w = u % 2
                pe.wait_ge(s_hh, k + 1)
                ins = te.transpose(ps[:, w * CH:w * CH + P], hh[:, w, :], ident[:, :])
                if left > 3:
                    ins = tokens_in(k + 3, (u + 3) % 4, w, need)
                ins.then_inc(s_hxt, 1)
                if left > 2:
                    gate_up(k + 2, w)
                e = expert_of(k)
                pe.wait_ge(s_hx, k + 4)
                te.matmul(bank(4 + w, D), hx[:, w, 0, :], w_dn[:, bass.ds(e, 1), :].rearrange("p o f -> p (o f)"),
                          start=True, stop=True).then_inc(s_dn, 1)

            def first_scores(j, q, n):
                if type(n) is int and n in (0, QT // 2):
                    for side in range(2):
                        pe.wait_ge(s_first[side][n // (QT // 2)][0], LOADS * DMA)
                if type(n) is not int or n > 0:
                    pe.wait_ge(s_ff, n)
                w = (q + 1) * P
                qq = qs[0:K_MAX, 0, bass.ds(j, 1), q * P:(q + 1) * P].rearrange("p j s -> p (j s)")
                for c in range(0, w, CH):
                    e = min(w, c + CH)
                    te.matmul(ps[:, 6 * CH + c:6 * CH + e], qq,
                              ks[0:K_MAX, 0, bass.ds(j, 1), c:e].rearrange("p j s -> p (j s)"), start=True, stop=e < w)
                te.matmul(ps[:, 6 * CH + w - P:6 * CH + w], idb, mask_q, start=False, stop=True).then_inc(s_fr, 1)

            def tile_steps(j, last):
                k = j * NTH
                for u in range(NTH):
                    tile_step(k + u, u, NTH - u if last else NT, (j * (NTH // 4) + (u + 3) // 4 + 1) * DMA)
                    for q in range(QT):
                        if FIRST_AT[q] == u:
                            first_scores(j, q, j * QT + q)

            pe.wait_ge(s_sha, 2)
            for k in range(2):
                tokens_in(k, k, (k + 1) % 2, DMA).then_inc(s_hxt, 1)
            pe.wait_ge(s_sha, TT // 2)
            pe.wait_ge(s_wgu, DMA)
            pe.wait_ge(s_wdn, DMA)
            for k in range(2):
                pe.wait_ge(s_hx, k + 1)
                gate_up(k, k)
            tokens_in(2, 2, 1, DMA).then_inc(s_hxt, 1)
            pe.wait_ge(s_hx, 3)
            tile_steps(0, False)
            with pe.Fori(1, HG - 1) as j:
                tile_steps(j, False)
            tile_steps(HG - 1, True)
            pe.wait_ge(s_ff, HG * QT)
            te.transpose(bank(6, P, HG * QT), mx[:, 0, :], ident[:, :]).then_inc(s_fr, 1)
            pe.wait_ge(s_yo, NT)
            pe.wait_ge(s_ff, HG * QT + 1)

            def max_scores(g, par, p):
                pe.wait_ge(s_mxf, (g - 1) * NP + p + 1)
                base = (4 + 2 * (p % 2)) * CH
                if p == NP - 1:
                    pe.wait_ge(s_mxf, MX_CREDIT + g * NP - 1)
                    te.transpose(bank(6, P, HG * QT), mx[:, par, :], ident[:, :]).then_inc(s_mxr, 1)
                    return
                qt, j0, nj = PIECES[p]
                w = (qt + 1) * P
                for j in range(j0, j0 + nj):
                    at = base + (j - j0) * w
                    q = qs[0:K_MAX, par, j, qt * P:(qt + 1) * P]
                    for c in range(0, w, CH):
                        e = min(w, c + CH)
                        te.matmul(ps[:, at + c:at + e], q, ks[0:K_MAX, par, j, c:e], start=True, stop=e < w)
                    ins = te.matmul(ps[:, at + w - P:at + w], idb, mask_q, start=False, stop=True)
                ins.then_inc(s_mxr, 1)

            def exp_scores(g, s, par, heads):
                qc, kb = STEPS[s]
                lo = max(0, kb * P - qc * CH)
                diag = kb * P >= qc * CH
                for j in heads:
                    n = HG * s + j
                    pe.wait_ge(s_exp, g * (HG * NS) + n + 1)
                    out = bank(n % 3)
                    ins = te.matmul(out[:, lo:CH], ks[0:K_EXP, par, j, kb * P:(kb + 1) * P],
                                    qs[0:K_EXP, par, j, qc * CH + lo:(qc + 1) * CH], start=True, stop=not diag)
                    if diag:
                        ins = te.matmul(out[:, lo:lo + P], idb, mask_k, start=False, stop=True)
                    ins.then_inc(s_st, 1)

            def weigh(g, s, par):
                qc, kb = STEPS[s]
                lo = max(0, kb * P - qc * CH)
                pe.wait_ge(s_exp, EXP_CREDIT + g * (HG * NS) + HG * (s + 1))
                if kb == 0:
                    pe.wait_ge(s_ev, g * 2 + qc + 1)
                for j in range(HG):
                    ins = te.matmul(ps[32 * j:32 * j + 32, OUT_BANK * CH + lo:(OUT_BANK + 1) * CH], vg[:, par, kb, j, :],
                                    pt[:, s % 2, j, lo:CH], start=kb == 0, stop=kb == 4 * qc + 3,
                                    tile_position=(0, 32 * j))
                ins.then_inc(s_pv, 1)


            def final(m):
                kind, n = FINAL[m]
                if m == 0:
                    pe.wait_ge(s_mxf, MX_CREDIT + (NG - 1) * NP)
                if m >= 4:
                    pe.wait_ge(s_inv, m - 3)
                if kind == "divide":
                    pe.wait_ge(s_invd[n // 2], 3 * DMA)
                    ins = te.matmul(bank(4 + m % 4), sel[:, :], inv[:, n // 2, n % 2 * CH:(n % 2 + 1) * CH],
                                    start=True, stop=True)
                else:
                    if n % QT == 0:
                        pe.wait_ge(s_inv, FINAL.index(("divide", NG * (n // QT + 1) - 1)) + 1)
                    for hg in range(H // HG):
                        ins = te.matmul(bank(4 + m % 4, D), ot[:, n // QT * 4 + hg, n % QT * P:(n % QT + 1) * P],
                                        wo_t[:, hg, :], start=hg == 0, stop=hg == 3)
                ins.then_inc(s_fin, 1)

            def pair(g, last, count):
                beside = 0
                for par in range(2):
                    pe.wait_ge(s_nl[par], count * (3 * DMA))
                    pe.wait_ge(s_vg, g + par + 1)
                    for kind, a, b in [(*x, 0)[:3] for x in ORDER]:
                        if kind == "exp":
                            exp_scores(g + par, a, par, [b])
                            if last and par:
                                while beside * HG * NS < (HG * a + b - 6) * BESIDE:
                                    final(beside)
                                    beside += 1
                        elif kind == "out" and a + par:
                            weigh(g + par - (a == 0), (a - 1) % NS, par - (a == 0))
                        elif kind == "max" and not (last and a + par > 1):
                            q = (par + a) % 2
                            if b in (0, FIRST_HALF):
                                for side in range(2):
                                    pe.wait_ge(s_ld[side][int(b > 0)][q], (count + (par + a) // 2) * (LOADS * DMA))
                            max_scores(g + par + a, q, b)
                weigh(g + 1, NS - 1, 1)
                return beside

            for side in range(2):
                for half in range(2):
                    pe.wait_ge(s_first[side][half][1], LOADS * DMA)
            for p in range(EARLY):
                max_scores(1, 1, p)
            with pe.Fori(0, NG // 2 - 1) as i:
                pair(i * 2, False, i + 1)
            beside = pair(NG - 2, True, NG // 2)

            for m in range(beside, len(FINAL)):
                final(m)


NAMES = {
    "L0_attn_hidden_states": "x", "L0_attn_qkv_w": "qkv_w", "L0_attn_qkv_b": "qkv_b", "L0_attn_out_w": "out_w",
    "L0_attn_out_b": "out_b", "L0_attn_alibi_slopes": "slopes", "L0_ffn_gate_w": "gate_w",
    "L0_ffn_expert_bias": "ebias", "L0_ffn_shared_gate_w": "sg_w", "L0_ffn_shared_up_w": "su_w",
    "L0_ffn_shared_down_w": "sd_w", "L0_ffn_experts_gate_up": "e_gu", "L0_ffn_experts_down": "e_dn",
}


def kernel(**inputs):
    import concourse.bacc as bacc
    from concourse.bass_utils import run_bass_kernel_spmd

    nc = bacc.Bacc("TRN2", target_bir_lowering=False, num_devices=1)
    arrays = {short: np.ascontiguousarray(inputs[name]) for name, short in NAMES.items()}
    arrays.update(constants())
    args = [nc.dram_tensor(k, a.shape, mybir.dt.from_np(a.dtype), kind="ExternalInput").ap()
            for k, a in arrays.items()]
    out = nc.dram_tensor("y", (B, S, D), F32, kind="ExternalOutput").ap()
    build(nc, *args, out)
    return run_bass_kernel_spmd(nc, [arrays], core_ids=[0]).results[0]["y"]
```
